# Optimizing a Trainium2 kernel written in Bass

```python
import numpy as np
import jax
import jax.numpy as jnp

def _softmax(x, axis=-1):
    return jax.nn.softmax(x, axis=axis)

def _gelu(x):
    return jax.nn.gelu(x, approximate=True)

def _silu(x):
    return jax.nn.silu(x)

def _sigmoid(x):
    return jax.nn.sigmoid(x)

def _layernorm(x, axis=-1, eps=1e-05):
    m = jnp.mean(x, axis=axis, keepdims=True)
    v = jnp.var(x, axis=axis, keepdims=True)
    return (x - m) / jnp.sqrt(v + eps)

def _scatter_add(tgt, idx, src, axis=0):
    return tgt.at[idx].add(src)

def _segment_sum(src, seg, n):
    return jax.ops.segment_sum(src, seg, n)
kernel_name = 'mk_dlrm_tower_d1_rec_r8_0a893f'

def setup_inputs(seed: int=0):
    np.random.seed(seed)
    _w = jnp.asarray

    def _rec_inputs():
        import jax
        import jax.numpy as jnp
        _tk = jax.random.key(seed)
        dense_ctx = jax.random.normal(jax.random.fold_in(_tk, 190), (1024, 16), jnp.float32)
        ids = jnp.stack([jax.random.randint(jax.random.fold_in(_tk, 200 + f), (1024,), 0, v, jnp.int32) for f, v in enumerate([12500, 125000, 1250, 125000, 1000, 1250, 1000, 125000, 1250, 1250, 12500, 125000, 125000, 1000, 1000, 1250, 1250, 12500, 1250, 1250, 125000, 125000, 12500, 1250, 1000, 1000])], axis=1)
        tbl_0 = 0.05 * jax.random.normal(jax.random.fold_in(_tk, 500 + 0), (12500, 32), jnp.float32)
        tbl_1 = 0.05 * jax.random.normal(jax.random.fold_in(_tk, 500 + 1), (125000, 32), jnp.float32)
        tbl_2 = 0.05 * jax.random.normal(jax.random.fold_in(_tk, 500 + 2), (1250, 32), jnp.float32)
        tbl_3 = 0.05 * jax.random.normal(jax.random.fold_in(_tk, 500 + 3), (125000, 32), jnp.float32)
        tbl_4 = 0.05 * jax.random.normal(jax.random.fold_in(_tk, 500 + 4), (1000, 32), jnp.float32)
        tbl_5 = 0.05 * jax.random.normal(jax.random.fold_in(_tk, 500 + 5), (1250, 32), jnp.float32)
        tbl_6 = 0.05 * jax.random.normal(jax.random.fold_in(_tk, 500 + 6), (1000, 32), jnp.float32)
        tbl_7 = 0.05 * jax.random.normal(jax.random.fold_in(_tk, 500 + 7), (125000, 32), jnp.float32)
        tbl_8 = 0.05 * jax.random.normal(jax.random.fold_in(_tk, 500 + 8), (1250, 32), jnp.float32)
        tbl_9 = 0.05 * jax.random.normal(jax.random.fold_in(_tk, 500 + 9), (1250, 32), jnp.float32)
        tbl_10 = 0.05 * jax.random.normal(jax.random.fold_in(_tk, 500 + 10), (12500, 32), jnp.float32)
        tbl_11 = 0.05 * jax.random.normal(jax.random.fold_in(_tk, 500 + 11), (125000, 32), jnp.float32)
        tbl_12 = 0.05 * jax.random.normal(jax.random.fold_in(_tk, 500 + 12), (125000, 32), jnp.float32)
        tbl_13 = 0.05 * jax.random.normal(jax.random.fold_in(_tk, 500 + 13), (1000, 32), jnp.float32)
        tbl_14 = 0.05 * jax.random.normal(jax.random.fold_in(_tk, 500 + 14), (1000, 32), jnp.float32)
        tbl_15 = 0.05 * jax.random.normal(jax.random.fold_in(_tk, 500 + 15), (1250, 32), jnp.float32)
        tbl_16 = 0.05 * jax.random.normal(jax.random.fold_in(_tk, 500 + 16), (1250, 32), jnp.float32)
        tbl_17 = 0.05 * jax.random.normal(jax.random.fold_in(_tk, 500 + 17), (12500, 32), jnp.float32)
        tbl_18 = 0.05 * jax.random.normal(jax.random.fold_in(_tk, 500 + 18), (1250, 32), jnp.float32)
        tbl_19 = 0.05 * jax.random.normal(jax.random.fold_in(_tk, 500 + 19), (1250, 32), jnp.float32)
        tbl_20 = 0.05 * jax.random.normal(jax.random.fold_in(_tk, 500 + 20), (125000, 32), jnp.float32)
        tbl_21 = 0.05 * jax.random.normal(jax.random.fold_in(_tk, 500 + 21), (125000, 32), jnp.float32)
        tbl_22 = 0.05 * jax.random.normal(jax.random.fold_in(_tk, 500 + 22), (12500, 32), jnp.float32)
        tbl_23 = 0.05 * jax.random.normal(jax.random.fold_in(_tk, 500 + 23), (1250, 32), jnp.float32)
        tbl_24 = 0.05 * jax.random.normal(jax.random.fold_in(_tk, 500 + 24), (1000, 32), jnp.float32)
        tbl_25 = 0.05 * jax.random.normal(jax.random.fold_in(_tk, 500 + 25), (1000, 32), jnp.float32)
        _rk = jax.random.fold_in(_tk, 7)
        W_top1 = 0.0606339 * jax.random.normal(jax.random.fold_in(_tk, 801), (272, 512), jnp.float32)
        W_top2 = 0.0441942 * jax.random.normal(jax.random.fold_in(_tk, 802), (512, 256), jnp.float32)
        W_top3 = 0.0625 * jax.random.normal(jax.random.fold_in(_tk, 803), (256, 1), jnp.float32)
        b_top1 = jnp.zeros((512,), jnp.float32)
        b_top2 = jnp.zeros((256,), jnp.float32)
        return (dense_ctx, ids, tbl_0, tbl_1, tbl_2, tbl_3, tbl_4, tbl_5, tbl_6, tbl_7, tbl_8, tbl_9, tbl_10, tbl_11, tbl_12, tbl_13, tbl_14, tbl_15, tbl_16, tbl_17, tbl_18, tbl_19, tbl_20, tbl_21, tbl_22, tbl_23, tbl_24, tbl_25, W_top1, b_top1, W_top2, b_top2, W_top3)
    dense_ctx, ids, tbl_0, tbl_1, tbl_2, tbl_3, tbl_4, tbl_5, tbl_6, tbl_7, tbl_8, tbl_9, tbl_10, tbl_11, tbl_12, tbl_13, tbl_14, tbl_15, tbl_16, tbl_17, tbl_18, tbl_19, tbl_20, tbl_21, tbl_22, tbl_23, tbl_24, tbl_25, W_top1, b_top1, W_top2, b_top2, W_top3 = _rec_inputs()

    def _L0_rec_setup():
        import jax, jax.numpy as jnp
        import numpy as np
        M_FIELDS = 26
        H1 = 128
        H2 = 128
        BATCH = 256
        EMB_K = 32

        def _cin_layer(x_prev, x0, W, b):
            return jnp.einsum('bik,bjk,hij->bhk', x_prev, x0, W) + b[None, :, None]
        key = jax.random.key(seed)
        k0, k1, k2, k3, k4 = jax.random.split(key, 5)
        inputs = jax.random.normal(k0, (BATCH, M_FIELDS, EMB_K), dtype=jnp.float32)
        W1 = jax.random.normal(k1, (H1, M_FIELDS, M_FIELDS), dtype=jnp.float32) * 0.05
        b1 = jax.random.normal(k2, (H1,), dtype=jnp.float32) * 0.05
        W2 = jax.random.normal(k3, (H2, H1, M_FIELDS), dtype=jnp.float32) * 0.05
        b2 = jax.random.normal(k4, (H2,), dtype=jnp.float32) * 0.05
        return {'inputs': inputs, 'W1': W1, 'b1': b1, 'W2': W2, 'b2': b2}
    _L0_rec_all = _L0_rec_setup()
    _L0_rec_in = {k: v for k, v in _L0_rec_all.items() if k in ('W1', 'b1', 'W2', 'b2')}
    del _L0_rec_all
    return {'dense_ctx': dense_ctx, 'ids': ids, 'tbl_0': tbl_0, 'tbl_1': tbl_1, 'tbl_2': tbl_2, 'tbl_3': tbl_3, 'tbl_4': tbl_4, 'tbl_5': tbl_5, 'tbl_6': tbl_6, 'tbl_7': tbl_7, 'tbl_8': tbl_8, 'tbl_9': tbl_9, 'tbl_10': tbl_10, 'tbl_11': tbl_11, 'tbl_12': tbl_12, 'tbl_13': tbl_13, 'tbl_14': tbl_14, 'tbl_15': tbl_15, 'tbl_16': tbl_16, 'tbl_17': tbl_17, 'tbl_18': tbl_18, 'tbl_19': tbl_19, 'tbl_20': tbl_20, 'tbl_21': tbl_21, 'tbl_22': tbl_22, 'tbl_23': tbl_23, 'tbl_24': tbl_24, 'tbl_25': tbl_25, 'W_top1': W_top1, 'b_top1': b_top1, 'W_top2': W_top2, 'b_top2': b_top2, 'W_top3': W_top3, 'L0_rec_W1': _L0_rec_in['W1'], 'L0_rec_b1': _L0_rec_in['b1'], 'L0_rec_W2': _L0_rec_in['W2'], 'L0_rec_b2': _L0_rec_in['b2']}

def reference(dense_ctx, ids, tbl_0, tbl_1, tbl_2, tbl_3, tbl_4, tbl_5, tbl_6, tbl_7, tbl_8, tbl_9, tbl_10, tbl_11, tbl_12, tbl_13, tbl_14, tbl_15, tbl_16, tbl_17, tbl_18, tbl_19, tbl_20, tbl_21, tbl_22, tbl_23, tbl_24, tbl_25, W_top1, b_top1, W_top2, b_top2, W_top3, L0_rec_W1, L0_rec_b1, L0_rec_W2, L0_rec_b2):
    import jax
    import jax.numpy as jnp

    def _L0_rec_ref(inputs, W1, b1, W2, b2):
        import jax, jax.numpy as jnp
        import numpy as np
        M_FIELDS = 26
        H1 = 128
        H2 = 128
        BATCH = 256
        EMB_K = 32

        def _cin_layer(x_prev, x0, W, b):
            return jnp.einsum('bik,bjk,hij->bhk', x_prev, x0, W) + b[None, :, None]
        x1 = _cin_layer(inputs, inputs, W1, b1)
        x2 = _cin_layer(x1, inputs, W2, b2)
        res = jnp.concatenate([x1, x2], axis=1)
        return jnp.sum(res, axis=-1)
    e = jnp.stack([tbl_0[ids[:, 0]], tbl_1[ids[:, 1]], tbl_2[ids[:, 2]], tbl_3[ids[:, 3]], tbl_4[ids[:, 4]], tbl_5[ids[:, 5]], tbl_6[ids[:, 6]], tbl_7[ids[:, 7]], tbl_8[ids[:, 8]], tbl_9[ids[:, 9]], tbl_10[ids[:, 10]], tbl_11[ids[:, 11]], tbl_12[ids[:, 12]], tbl_13[ids[:, 13]], tbl_14[ids[:, 14]], tbl_15[ids[:, 15]], tbl_16[ids[:, 16]], tbl_17[ids[:, 17]], tbl_18[ids[:, 18]], tbl_19[ids[:, 19]], tbl_20[ids[:, 20]], tbl_21[ids[:, 21]], tbl_22[ids[:, 22]], tbl_23[ids[:, 23]], tbl_24[ids[:, 24]], tbl_25[ids[:, 25]]], axis=1)
    z = _L0_rec_ref(e, L0_rec_W1, L0_rec_b1, L0_rec_W2, L0_rec_b2)
    z = z.reshape(z.shape[0], -1)
    h = jnp.concatenate([z, dense_ctx], axis=1)
    h = jnp.maximum(h @ W_top1 + b_top1, 0.0)
    h = jnp.maximum(h @ W_top2 + b_top2, 0.0)
    y = h @ W_top3
    return y

_drawn_inputs = setup_inputs


def setup_inputs(seed=0):
    import zlib

    import numpy as np

    out = dict(_drawn_inputs(seed))
    spreads = {'b_top1': (0.0, 2.0), 'b_top2': (0.0, 0.8)}
    factors = {'tbl_0': 8.0,
     'tbl_1': 8.0,
     'tbl_2': 8.0,
     'tbl_3': 8.0,
     'tbl_4': 8.0,
     'tbl_5': 8.0,
     'tbl_6': 8.0,
     'tbl_7': 8.0,
     'tbl_8': 8.0,
     'tbl_9': 8.0,
     'tbl_10': 8.0,
     'tbl_11': 8.0,
     'tbl_12': 8.0,
     'tbl_13': 8.0,
     'tbl_14': 8.0,
     'tbl_15': 8.0,
     'tbl_16': 8.0,
     'tbl_17': 8.0,
     'tbl_18': 8.0,
     'tbl_19': 8.0,
     'tbl_20': 8.0,
     'tbl_21': 7.624,
     'tbl_22': 8.0,
     'tbl_23': 8.0,
     'tbl_24': 8.0,
     'tbl_25': 8.0,
     'L0_rec_W1': 7.859,
     'L0_rec_W2': 4.29,
     'dense_ctx': 5.813}
    for name, (base, spread) in spreads.items():
        noise = np.random.default_rng([zlib.crc32(name.encode()), seed]).standard_normal(out[name].shape)
        drawn = base * np.exp(spread * noise) if base else spread * noise
        out[name] = jnp.asarray(drawn.astype(out[name].dtype))
    for name, factor in factors.items():
        out[name] = (out[name] * factor).astype(out[name].dtype)
    return out
```

```python
from contextlib import ExitStack

import numpy as np

import concourse.bass as bass
from concourse import mybir

F32 = mybir.dt.float32
I32 = mybir.dt.int32
ALU = mybir.AluOpType
ACT = mybir.ActivationFunctionType

P = 128
B = 1024
F = 26
HALF = F // 2
K = 32
H = 128
D = 16
N1, N2 = 512, 256
GROUP = 2 * P
GROUPS = B // GROUP
U_HALF = 16
FOUR = 4
EVAC = 4

MCOLS = F + 2


def tri(fields):
    fields = list(fields)
    return [(p, q) for n, p in enumerate(fields) for q in fields[n + 1:]]


def rect(first, second):
    return [(p, q) for p in first for q in second]


PART_A = [("single", f) for f in range(HALF)] + rect(range(0, 5), range(5, 13)) + rect(range(5, 10), range(10, 13)) \
    + tri(range(10, 13))
PART_S = [(f, f) for f in range(F)] + tri(range(0, 5)) + tri(range(5, 10)) + tri(range(19, 23)) \
    + tri(range(23, 26)) + ["one"]
PART_B = rect(range(13, 19), range(19, 26)) + tri(range(13, 19)) + rect(range(19, 23), range(23, 26))
ROWS = PART_A + PART_S + PART_B
R0 = (0, len(PART_A))
RN = (len(PART_A) + len(PART_S), len(PART_S) + len(PART_B))
ONE_ROW = len(PART_A) + len(PART_S) - 1
J0 = (10, 0)
JN = (16, 19)
C0 = (J0[0] + 1, 0)
CN = (JN[0] + 1, JN[1] + 1)
TCOLS = sum(CN)
T0 = (0, CN[0])
TJ = (0, CN[0] + 1)
TONE = (JN[0], CN[0])
VN = sum(JN)
V0 = (0, JN[0])
UROWS = 2 * HALF * HALF


def plan():
    mult = np.zeros((P, VN), np.float32)
    zmult = np.zeros((P, 2), np.float32)
    index = np.full((P, 4), UROWS, np.int32)
    seen, pairs, ones = set(), set(), set()
    for c in range(2):
        for r, row in enumerate(ROWS[R0[c]:R0[c] + RN[c]]):
            for j in range(J0[c], J0[c] + JN[c]):
                if row == "one":
                    if j not in ones:
                        ones.add(j)
                        mult[r, V0[c] + j - J0[c]] = 1.0
                elif row[0] != "single":
                    key = tuple(sorted(row + (j,)))
                    if key not in seen:
                        seen.add(key)
                        mult[r, V0[c] + j - J0[c]] = (1.0, 0.5, 1.0 / 6.0)[3 - len(set(key))]
            if row != "one" and row[0] != "single":
                p, q = row
                index[r, 2 * c] = p * HALF + q % HALF
                index[r, 2 * c + 1] = q * HALF + p % HALF
                if row not in pairs:
                    pairs.add(row)
                    zmult[r, c] = 0.5 if p == q else 1.0
    assert len(seen) == F * (F + 1) * (F + 2) // 6 and len(ones) == F
    assert len(pairs) == 2 * (HALF * (HALF + 1) // 2)
    return mult, zmult, index


SMALL = [
    ("w1a", [P, 2 * P]), ("w1b", [P, 2 * P]), ("mult", [P, VN]), ("zmult", [P, 2]), ("z1a", [P, 2 * H]),
    ("z1b", [P, 2 * H]), ("xa", [HALF, HALF * H]), ("xb", [HALF, HALF * H]), ("cin_b", [P, 2]),
    ("b_top1", [P, N1 // P]), ("b_top2", [P, N2 // P]), ("top1", [P, 2 * N1]), ("top1d", [D, N1]),
    ("top2", [P, N1 // P * N2]), ("top3", [P, N2 // P]), ("dense", [D, B]),
]


def build(nc, io, tables, out):
    with ExitStack() as ctx:
        def sb(name, shape, dt=F32):
            return ctx.enter_context(nc.sbuf_tensor(name, shape, dt))

        def sem(name):
            return ctx.enter_context(nc.semaphore(name))

        idx = [sb(f"idx{n}", [P, F], I32) for n in range(2)]
        rows = [sb(f"rows{n}", [P, F * K]) for n in range(2)]
        emb = [sb(f"emb{n}", [P, 2 * U_HALF, F]) for n in range(2)]
        mov = [sb(f"mov{n}", [P, U_HALF, FOUR, MCOLS]) for n in range(2)]
        prod = [sb(f"prod{n}", [P, U_HALF, len(ROWS)]) for n in range(2)]
        T = sb("T", [P, 2, TCOLS, P])
        V = sb("V", [P, VN * H])
        w1 = sb("w1", [P, F * F])
        w1f = sb("w1f", [P, F * F])
        w2 = sb("w2", [P, F * H])
        vidx = sb("vidx", [P, 4], I32)
        scratch = sb("scratch", [P, 2 * VN * H])
        other = [[scratch[:, 2 * V0[c] * H + t * JN[c] * H:][:, 0:JN[c] * H] for t in range(2)] for c in range(2)]
        stage = [scratch[:, n * HALF * H:(n + 1) * HALF * H] for n in range(4)]
        zero = sb("zero", [F, H])
        small = {name: sb(f"s_{name}", shape) for name, shape in SMALL}
        cin_bk = sb("cin_bk", [P, 2])
        z = sb("z", [P, 2, GROUP])
        h1 = sb("h1", [P, N1 // P, GROUP])
        h2 = sb("h2", [P, N2 // P, GROUP])
        y = sb("y", [1, B])

        def bank(name):
            return ctx.enter_context(nc.psum_tensor(name, [P, 512], F32))

        tps = [bank(f"tps{n}") for n in range(4)]
        zps = [bank(f"zps{n}") for n in range(2)]
        mps = [bank(f"mps{n}") for n in range(2)]

        udram = nc.dram_tensor("udram", [UROWS + 1, F * H], F32, kind="Internal").ap()

        idx_loaded = [sem(f"idx_loaded{n}") for n in range(2)]
        w12_loaded = sem("w12_loaded")
        small_loaded = sem("small_loaded")
        gather_begun = sem("gather_begun")
        vidx_loaded = sem("vidx_loaded")
        gathered = [sem(f"gathered{n}") for n in range(2)]
        emb_ready = [sem(f"emb_ready{n}") for n in range(2)]
        prod_ready = [sem(f"prod_ready{n}") for n in range(2)]
        mov_ready = [sem(f"mov_ready{n}") for n in range(2)]
        half_used = [sem(f"half_used{n}") for n in range(2)]
        tps_full = [sem(f"tps_full{n}") for n in range(4)]
        tps_free = [sem(f"tps_free{n}") for n in range(4)]
        zeroed = sem("zeroed")
        preset = sem("preset")
        w1f_ready = sem("w1f_ready")
        w1r_ready = sem("w1r_ready")
        zw_ready = sem("zw_ready")
        pre_full = sem("pre_full")
        pre_free = sem("pre_free")
        u_written = [sem(f"u_written{n}") for n in range(4)]
        uzero_written = sem("uzero_written")
        v_gathered = sem("v_gathered")
        v_step = sem("v_step")
        v_ready = sem("v_ready")
        z_full = sem("z_full")
        z_ready = sem("z_ready")
        h_full = sem("h_full")
        h_ready = sem("h_ready")
        y_stored = sem("y_stored")

        block = ctx.enter_context(nc.Block())

        USTAGES = [(g, p, min(4, HALF - p)) for g in range(2) for p in range(0, HALF, 4)]
        UQ = [(q, min(4, HALF - q)) for q in range(0, HALF, 4)]
        VSTEPS = [(c, j, min(4, JN[c] - j)) for c in range(2) for j in range(0, JN[c], 4)]
        PRE = len(USTAGES) * len(UQ) + len(VSTEPS)
        WRITES = [sum(USTAGES[s][2] for s in range(b, len(USTAGES), 4)) for b in range(4)]

        @block.sync
        def _(sp):
            sp.dma_start(idx[0][:], io["ids"][0:P, :]).then_inc(idx_loaded[0], 16)
            sp.dma_start(idx[1][:], io["ids"][P:2 * P, :]).then_inc(idx_loaded[1], 16)
            sp.dma_start(w1[:], io["w1"]).then_inc(w12_loaded, 16)
            sp.dma_start(w2[:], io["w2"]).then_inc(w12_loaded, 16)
            sp.dma_start(vidx[:], io["vidx"]).then_inc(vidx_loaded, 16)
            for name, _ in SMALL:
                sp.dma_start(small[name][:], io[name]).then_inc(small_loaded, 16)
            sp.wait_ge(zeroed, 1)
            sp.dma_start(udram[UROWS:UROWS + 1, :].rearrange("o (j h) -> (o j) h", h=H), zero[:]).then_inc(uzero_written, 16)
            for s, (g, p0, n) in enumerate(USTAGES):
                sp.wait_ge(pre_free, len(UQ) * (s + 1))
                for p in range(n):
                    row = (g * HALF + p0 + p) * HALF
                    dst = udram[row:row + HALF, :].rearrange("q (j h) -> j q h", h=H)
                    src = stage[s % 4][p * F:(p + 1) * F, :].rearrange("j (q h) -> j q h", h=H)
                    sp.dma_start(dst, src).then_inc(u_written[s % 4], 16)
            with sp.Fori(1, GROUPS) as it:
                for par in range(2):
                    sp.wait_ge(gathered[par], it * (16 * F))
                    sp.dma_start(idx[par][:], io["ids"][bass.ds(it * GROUP + par * P, P), :]).then_inc(idx_loaded[par], 16)

        @block.gpsimd
        def _(pool):
            def gather_tile(it, par):
                pool.wait_ge(idx_loaded[par], 16 * (it + 1))
                pool.wait_ge(emb_ready[par], it + 1)
                pool.sem_inc(gather_begun, 1)
                for f in range(F):
                    nc.gpsimd.indirect_dma_start(
                        out=rows[par][:, f * K:(f + 1) * K], out_offset=None, in_=tables[f],
                        in_offset=bass.IndirectOffsetOnAxis(ap=idx[par][:, f:f + 1], axis=0),
                    ).then_inc(gathered[par], 16)

            for par in range(2):
                gather_tile(0, par)
            pool.wait_ge(vidx_loaded, 16)
            pool.wait_ge(uzero_written, 16)
            for b in range(4):
                pool.wait_ge(u_written[b], 16 * WRITES[b])
            for c in range(2):
                for t in range(2):
                    nc.gpsimd.indirect_dma_start(
                        out=other[c][t][0:RN[c], :], out_offset=None, in_=udram,
                        in_offset=bass.IndirectOffsetOnAxis(ap=vidx[0:RN[c], 2 * c + t:2 * c + t + 1], axis=0),
                        element_offset=J0[c] * H,
                    ).then_inc(v_gathered, 16)
            with pool.Fori(1, GROUPS) as it:
                for par in range(2):
                    gather_tile(it, par)

        @block.vector
        def _(dve):
            for par in range(2):
                dve.sem_inc(emb_ready[par], 1)
            nc.vector.memset(zero[:], 0.0).then_inc(zeroed, 1)
            for n in range(2):
                last = nc.vector.memset(mov[n][:], 0.0)
            last.then_inc(zeroed, 1)
            dve.wait_ge(zeroed, 2)
            for n in range(2):
                for g in range(FOUR):
                    for col in (0, MCOLS - 1):
                        nc.vector.memset(mov[n][g * K:(g + 1) * K, :, g, col:col + 1], 1.0)
                last = nc.vector.memset(prod[n][:, :, ONE_ROW:ONE_ROW + 1], 1.0)
            last.then_inc(preset, 1)
            dve.wait_ge(w12_loaded, 32)
            a = w1[:].rearrange("i (p q) -> i p q", q=F)
            nc.vector.tensor_tensor(w1f[:].rearrange("i (p q) -> i p q", q=F), a, w1[:].rearrange("i (q p) -> i p q", p=F),
                                    ALU.add).then_inc(w1f_ready, 1)
            dve.wait_ge(small_loaded, 16 * len(SMALL))
            nc.vector.tensor_tensor(small["w1a"][:], small["w1a"][:], small["w1b"][:], ALU.add).then_inc(w1r_ready, 1)
            nc.vector.tensor_tensor(small["z1a"][:], small["z1a"][:], small["z1b"][:], ALU.add).then_inc(zw_ready, 1)
            dve.wait_ge(zw_ready, 1)
            for c in range(2):
                part = small["z1a"][:, c * H:(c + 1) * H]
                nc.vector.tensor_scalar(part, part, small["zmult"][:, c:c + 1], None, ALU.mult)
            nc.vector.tensor_tensor(small["xa"][:], small["xa"][:], small["xb"][:], ALU.add)
            nc.vector.tensor_scalar(cin_bk[:], small["cin_b"][:], float(K), None, ALU.mult).then_inc(zw_ready, 1)

            def tile(it, par):
                n = 2 * it + par
                dve.wait_ge(gathered[par], (it + 1) * (16 * F))
                nc.vector.transpose(emb[par][:].rearrange("p u f -> p f u"),
                                    rows[par][:].rearrange("p (f k) -> p f k", k=K)).then_inc(emb_ready[par], 1)
                for h in range(2):
                    if h == 0:
                        dve.wait_ge(emb_ready[par], it + 2)
                    dve.wait_ge(half_used[h], n + 1)
                    e = emb[par][:, h * U_HALF:(h + 1) * U_HALF, :]
                    q = prod[h]

                    def rectangle(row, p0, np_, q0, nq):
                        shape = [P, U_HALF, np_, nq]
                        return nc.vector.tensor_tensor(
                            q[:, :, row:row + np_ * nq].rearrange("p u (a b) -> p u a b", b=nq),
                            e[:, :, p0:p0 + np_].unsqueeze(3).to_broadcast(shape),
                            e[:, :, q0:q0 + nq].unsqueeze(2).to_broadcast(shape), ALU.mult)

                    def triangle(row, p0, np_):
                        for p in range(np_ - 1):
                            w = np_ - 1 - p
                            nc.vector.tensor_tensor(
                                q[:, :, row:row + w], e[:, :, p0 + p:p0 + p + 1].to_broadcast([P, U_HALF, w]),
                                e[:, :, p0 + p + 1:p0 + np_], ALU.mult)
                            row += w

                    row = HALF
                    nc.vector.tensor_copy(q[:, :, 0:HALF], e[:, :, 0:HALF])
                    rectangle(row, 0, 5, 5, 8)
                    rectangle(row + 40, 5, 5, 10, 3)
                    triangle(row + 55, 10, 3)
                    row = R0[1]
                    nc.vector.tensor_tensor(q[:, :, row:row + F], e, e, ALU.mult)
                    row += F
                    for p0, np_ in ((0, 5), (5, 5), (19, 4), (23, 3)):
                        triangle(row, p0, np_)
                        row += np_ * (np_ - 1) // 2
                    row += 1
                    rectangle(row, 13, 6, 19, 7)
                    triangle(row + 42, 13, 6)
                    rectangle(row + 57, 19, 4, 23, 3).then_inc(prod_ready[h], 1)

            for par in range(2):
                tile(0, par)
            dve.wait_ge(v_gathered, 64)
            dve.wait_ge(pre_free, PRE)
            step = 0
            for c in range(2):
                n = RN[c]
                x, v = other[c][0][0:n, :], V[0:n, V0[c] * H:(V0[c] + JN[c]) * H]
                m = small["mult"][0:n, V0[c]:V0[c] + JN[c]].unsqueeze(2).to_broadcast([n, JN[c], H])
                v3 = v.rearrange("r (j h) -> r j h", h=H)
                nc.vector.tensor_tensor(x, x, other[c][1][0:n, :], ALU.add).then_inc(v_step, 1)
                dve.wait_ge(v_step, step + 1)
                nc.vector.tensor_tensor(v, v, x, ALU.add).then_inc(v_step, 1)
                dve.wait_ge(v_step, step + 2)
                nc.vector.tensor_tensor(v3, v3, m, ALU.mult).then_inc(v_ready, 1)
                step += 2
            with dve.Fori(1, GROUPS) as it:
                for par in range(2):
                    tile(it, par)

        @block.scalar
        def _(act):
            n = 0
            for s, (g, p0, np_) in enumerate(USTAGES):
                if s >= 4:
                    act.wait_ge(u_written[s % 4], 16 * USTAGES[s - 4][2])
                for q, nq in UQ:
                    act.wait_ge(pre_full, n + 1)
                    nc.scalar.copy(stage[s % 4][0:np_ * F, q * H:(q + nq) * H],
                                   tps[n % 4][0:np_ * F, 0:nq * H]).then_inc(pre_free, 1)
                    n += 1
            for c, j, nj in VSTEPS:
                act.wait_ge(pre_full, n + 1)
                nc.scalar.copy(V[0:RN[c], (V0[c] + j) * H:(V0[c] + j + nj) * H],
                               tps[n % 4][0:RN[c], 0:nj * H]).then_inc(pre_free, 1)
                n += 1
            for bk in range(4):
                act.sem_inc(tps_free[bk], 1)
            act.wait_ge(preset, 1)
            act.wait_ge(zw_ready, 2)

            def tile(it, par):
                n = 2 * it + par
                for h in range(2):
                    act.wait_ge(emb_ready[par], it + 2)
                    act.wait_ge(half_used[h], n + 1)
                    for g in range(FOUR):
                        last = nc.scalar.copy(mov[h][g * K:(g + 1) * K, :, g, 1:1 + F],
                                              emb[par][g * K:(g + 1) * K, h * U_HALF:(h + 1) * U_HALF, :])
                    last.then_inc(mov_ready[h], 1)
                for k in range(16):
                    c, u0, bk = k % 2, k // 2 * EVAC, k % 4
                    if k % 8 == 7:
                        act.wait_ge(half_used[k // 8], n + 2)
                    elif bk == 3:
                        act.wait_ge(tps_full[bk], 2 * n + (k // 8 + 1))
                    else:
                        act.wait_ge(tps_full[bk], 4 * n + (k // 4 + 1))
                    src = tps[bk][0:RN[c], 0:EVAC * FOUR * CN[c]].rearrange("r (u g c) -> r c g u", g=FOUR, c=CN[c])
                    dst = T[0:RN[c], par, T0[c]:T0[c] + CN[c], :].rearrange("r c (g u) -> r c g u", g=FOUR)
                    nc.scalar.copy(dst[:, :, :, u0:u0 + EVAC], src).then_inc(tps_free[bk], 1)

            with act.Fori(0, GROUPS) as it:
                for par in range(2):
                    tile(it, par)
                for s in range(2):
                    act.wait_ge(z_full, 2 * it + (s + 1))
                    nc.scalar.activation(z[:, s, :], zps[s][:, 0:GROUP], ACT.Identity,
                                         bias=cin_bk[:, s:s + 1]).then_inc(z_ready, 1)
                for s in range(7):
                    act.wait_ge(h_full, 7 * it + (s + 1))
                    src = mps[s % 2]
                    if s < 4:
                        nc.scalar.activation(h1[:, s, :], src[:, 0:GROUP], ACT.Relu,
                                             bias=small["b_top1"][:, s:s + 1]).then_inc(h_ready, 1)
                    elif s < 6:
                        nc.scalar.activation(h2[:, s - 4, :], src[:, 0:GROUP], ACT.Relu,
                                             bias=small["b_top2"][:, s - 4:s - 3]).then_inc(h_ready, 1)
                    else:
                        nc.scalar.copy(y[:, bass.ds(it * GROUP, GROUP)], src[0:1, 0:GROUP]).then_inc(h_ready, 1)
            act.wait_ge(h_ready, 7 * GROUPS)
            act.dma_start(out.rearrange("b o -> o b"), y[:]).then_inc(y_stored, 16)
            act.wait_ge(y_stored, 16)

        @block.tensor
        def _(pe):
            pe.wait_ge(w12_loaded, 32)
            for h in range(2):
                pe.sem_inc(half_used[h], 1)
            pe.wait_ge(w1f_ready, 1)
            n = 0
            for g, p0, np_ in USTAGES:
                for q, nq in UQ:
                    if n >= 4:
                        pe.wait_ge(pre_free, n - 3)
                    first = (g * HALF + q) * H
                    nc.tensor.matmul(tps[n % 4][0:np_ * F, 0:nq * H], w1f[:, (g * HALF + p0) * F:][:, 0:np_ * F],
                                     w2[:, first:first + nq * H], start=True, stop=True).then_inc(pre_full, 1)
                    n += 1
            pe.wait_ge(w1r_ready, 1)
            for c, j, nj in VSTEPS:
                pe.wait_ge(pre_free, n - 3)
                nc.tensor.matmul(tps[n % 4][0:RN[c], 0:nj * H], small["w1a"][:, c * P:c * P + RN[c]],
                                 w2[:, (J0[c] + j) * H:(J0[c] + j + nj) * H], start=True, stop=True).then_inc(pre_full, 1)
                n += 1
            pe.wait_ge(pre_free, PRE)
            pe.wait_ge(zw_ready, 2)

            def tile(it, par):
                n = 2 * it + par
                for h in range(2):
                    pe.wait_ge(mov_ready[h], n + 1)
                    pe.wait_ge(prod_ready[h], n + 1)
                    for k in range(8 * h, 8 * h + 8):
                        c, bk = k % 2, k % 4
                        pe.wait_ge(tps_free[bk], 4 * n + (k // 4 + 1))
                        w = FOUR * CN[c]
                        for v in range(EVAC):
                            u = k // 2 * EVAC + v - h * U_HALF
                            last = nc.tensor.matmul(
                                tps[bk][0:RN[c], v * w:(v + 1) * w], prod[h][:, u, R0[c]:R0[c] + RN[c]],
                                mov[h][:, u, :, C0[c]:C0[c] + CN[c]], start=True, stop=True)
                        last.then_inc(half_used[h] if k % 8 == 7 else tps_full[bk], 1)

            with pe.Fori(0, GROUPS) as it:
                for par in range(2):
                    tile(it, par)
                for bk in range(4):
                    pe.wait_ge(tps_free[bk], 8 * it + 9)
                for c in range(2):
                    nc.tensor.matmul(zps[0][:, 0:GROUP], small["z1a"][0:RN[c], c * H:(c + 1) * H],
                                     T[0:RN[c], :, TONE[c], :], start=(c == 0), stop=False)
                for q in range(HALF):
                    last = nc.tensor.matmul(zps[0][:, 0:GROUP], small["xa"][:, q * H:(q + 1) * H],
                                            T[0:HALF, :, TJ[0] + HALF - J0[0] + q, :], start=False, stop=(q == HALF - 1))
                last.then_inc(z_full, 1)
                pe.wait_ge(v_ready, 2)
                for c in range(2):
                    for j in range(JN[c]):
                        v = (V0[c] + j) * H
                        last = nc.tensor.matmul(zps[1][:, 0:GROUP], V[0:RN[c], v:v + H], T[0:RN[c], :, TJ[c] + j, :],
                                                start=(c == 0 and j == 0), stop=(c == 1 and j == JN[1] - 1))
                last.then_inc(z_full, 1)
                for s in range(7):
                    if s == 0:
                        pe.wait_ge(z_ready, 2 * it + 2)
                    elif s >= 2:
                        pe.wait_ge(h_ready, 7 * it + (4 if s == 4 else 6 if s == 6 else s - 1))
                    if s < 4:
                        for k in range(2):
                            nc.tensor.matmul(mps[s % 2][:, 0:GROUP], small["top1"][:, k * N1 + s * P:k * N1 + (s + 1) * P],
                                             z[:, k, :], start=(k == 0), stop=False)
                        last = nc.tensor.matmul(mps[s % 2][:, 0:GROUP], small["top1d"][:, s * P:(s + 1) * P],
                                                small["dense"][:, bass.ds(it * GROUP, GROUP)], start=False, stop=True)
                    elif s < 6:
                        for k in range(4):
                            w = k * N2 + (s - 4) * P
                            last = nc.tensor.matmul(mps[s % 2][:, 0:GROUP], small["top2"][:, w:w + P], h1[:, k, :],
                                                    start=(k == 0), stop=(k == 3))
                    else:
                        for k in range(2):
                            last = nc.tensor.matmul(mps[s % 2][0:1, 0:GROUP], small["top3"][:, k:k + 1], h2[:, k, :],
                                                    start=(k == 0), stop=(k == 1))
                    last.then_inc(h_full, 1)


def by_rows(first, second):
    idx = np.zeros((2, 2, P), np.int64)
    is_pair = np.zeros((2, P), bool)
    for c in range(2):
        for r, row in enumerate(ROWS[R0[c]:R0[c] + RN[c]]):
            if row != "one" and row[0] != "single":
                idx[0, c, r], idx[1, c, r] = row
                is_pair[c, r] = True
    return idx[first], idx[second], is_pair


def kernel(**inputs):
    import concourse.bacc as bacc
    from concourse.bass_utils import run_bass_kernel_spmd

    a = {k: np.asarray(v) for k, v in inputs.items()}
    W1, W2 = a["L0_rec_W1"], a["L0_rec_W2"]
    mult, zmult, index = plan()
    one = np.array([[r < RN[c] and ROWS[R0[c] + r] == "one" for r in range(P)] for c in range(2)])
    arrays = {"ids": a["ids"], "w1": W1.reshape(H, F * F), "w2": W2.transpose(1, 2, 0).reshape(H, F * H),
              "mult": mult, "zmult": zmult, "vidx": index}
    for name, order in (("a", (0, 1)), ("b", (1, 0))):
        p, q, is_pair = by_rows(*order)
        rows = np.where(is_pair[None], W1[:, p, q], np.float32(0))
        arrays["z1" + name] = rows.transpose(2, 1, 0).reshape(P, 2 * H)
        if name == "a":
            rows = np.where(one[None], a["L0_rec_b1"][:, None, None], rows)
        arrays["w1" + name] = rows.reshape(H, 2 * P)
    arrays["xa"] = W1[:, :HALF, HALF:].transpose(1, 2, 0).reshape(HALF, HALF * H)
    arrays["xb"] = W1[:, HALF:, :HALF].transpose(2, 1, 0).reshape(HALF, HALF * H)
    arrays["cin_b"] = np.stack([a["L0_rec_b1"], a["L0_rec_b2"]], axis=1)
    arrays["b_top1"] = a["b_top1"].reshape(N1 // P, P).T
    arrays["b_top2"] = a["b_top2"].reshape(N2 // P, P).T
    arrays["top1"] = a["W_top1"][:2 * H].reshape(2, P, N1).transpose(1, 0, 2).reshape(P, 2 * N1)
    arrays["top1d"] = a["W_top1"][2 * H:]
    arrays["top2"] = a["W_top2"].reshape(N1 // P, P, N2).transpose(1, 0, 2).reshape(P, -1)
    arrays["top3"] = a["W_top3"].reshape(N2 // P, P).T
    arrays["dense"] = a["dense_ctx"].T
    for f in range(F):
        arrays[f"tbl_{f}"] = a[f"tbl_{f}"]

    nc = bacc.Bacc("TRN2", target_bir_lowering=False, num_devices=1)
    maps, aps = {}, {}
    for name, x in arrays.items():
        x = np.ascontiguousarray(x)
        maps["in_" + name] = x
        aps[name] = nc.dram_tensor("in_" + name, x.shape, mybir.dt.from_np(x.dtype), kind="ExternalInput").ap()
    out = nc.dram_tensor("out", (B, 1), F32, kind="ExternalOutput").ap()
    build(nc, aps, [aps[f"tbl_{f}"] for f in range(F)], out)
    r = run_bass_kernel_spmd(nc, [maps], core_ids=[0])
    return r.results[0]["out"]
```

```python
from contextlib import ExitStack

import numpy as np

import concourse.bass as bass
from concourse import mybir

F32 = mybir.dt.float32
I32 = mybir.dt.int32
ALU = mybir.AluOpType
ACT = mybir.ActivationFunctionType

P = 128
B = 1024
F = 26
HALF = F // 2
K = 32
H = 128
D = 16
N1, N2 = 512, 256
TILES = B // P
U_HALF = 16
FOUR = 4
EVAC = 4

MCOLS = F + 2


def tri(fields):
    fields = list(fields)
    return [(p, q) for n, p in enumerate(fields) for q in fields[n + 1:]]


def rect(first, second):
    return [(p, q) for p in first for q in second]


PART_A = [("single", f) for f in range(HALF)] + rect(range(0, 5), range(5, 13)) + rect(range(5, 10), range(10, 13)) \
    + tri(range(10, 13))
PART_S = [(f, f) for f in range(F)] + tri(range(0, 5)) + tri(range(5, 10)) + tri(range(19, 23)) \
    + tri(range(23, 26)) + ["one"]
PART_B = rect(range(13, 19), range(19, 26)) + tri(range(13, 19)) + rect(range(19, 23), range(23, 26))
ROWS = PART_A + PART_S + PART_B
R0 = (0, len(PART_A))
RN = (len(PART_A) + len(PART_S), len(PART_S) + len(PART_B))
ONE_ROW = len(PART_A) + len(PART_S) - 1
J0 = (10, 0)
JN = (16, 19)
C0 = (J0[0] + 1, 0)
CN = (JN[0] + 1, JN[1] + 1)
TCOLS = sum(CN)
T0 = (0, CN[0])
TJ = (0, CN[0] + 1)
TONE = (JN[0], CN[0])
VN = sum(JN)
V0 = (0, JN[0])
UROWS = 2 * HALF * HALF


def plan():
    mult = np.zeros((P, VN), np.float32)
    zmult = np.zeros((P, 2), np.float32)
    index = np.full((P, 4), UROWS, np.int32)
    seen, pairs, ones = set(), set(), set()
    for c in range(2):
        for r, row in enumerate(ROWS[R0[c]:R0[c] + RN[c]]):
            for j in range(J0[c], J0[c] + JN[c]):
                if row == "one":
                    if j not in ones:
                        ones.add(j)
                        mult[r, V0[c] + j - J0[c]] = 1.0
                elif row[0] != "single":
                    key = tuple(sorted(row + (j,)))
                    if key not in seen:
                        seen.add(key)
                        mult[r, V0[c] + j - J0[c]] = (1.0, 0.5, 1.0 / 6.0)[3 - len(set(key))]
            if row != "one" and row[0] != "single":
                p, q = row
                index[r, 2 * c] = p * HALF + q % HALF
                index[r, 2 * c + 1] = q * HALF + p % HALF
                if row not in pairs:
                    pairs.add(row)
                    zmult[r, c] = 0.5 if p == q else 1.0
    assert len(seen) == F * (F + 1) * (F + 2) // 6 and len(ones) == F
    assert len(pairs) == 2 * (HALF * (HALF + 1) // 2)
    return mult, zmult, index


XQ = ((0, 9), (9, HALF))

SMALL = [
    ("w1a", [P, 2 * P]), ("w1b", [P, 2 * P]), ("mult", [P, VN]), ("zmult", [P, 2]), ("z1a", [P, 2 * H]),
    ("z1b", [P, 2 * H]), ("xa", [P, 2 * H]), ("xb", [P, 2 * H]), ("cin_b", [P, 2]),
    ("b_top1", [P, N1 // P]), ("b_top2", [P, N2 // P]), ("top1", [P, 2 * N1]), ("top1d", [D, N1]),
    ("top2", [P, N1 // P * N2]), ("top3", [P, N2 // P]), ("dense", [D, B]),
]


def build(nc, io, tables, out):
    with ExitStack() as ctx:
        def sb(name, shape, dt=F32):
            return ctx.enter_context(nc.sbuf_tensor(name, shape, dt))

        def sem(name):
            return ctx.enter_context(nc.semaphore(name))

        idx = [sb(f"idx{n}", [P, F], I32) for n in range(2)]
        rows = [sb(f"rows{n}", [P, F * K]) for n in range(2)]
        emb = [sb(f"emb{n}", [P, 2 * U_HALF, F]) for n in range(2)]
        mov = [sb(f"mov{n}", [P, U_HALF, FOUR, MCOLS]) for n in range(2)]
        prod = [sb(f"prod{n}", [P, U_HALF, len(ROWS)]) for n in range(2)]
        T = sb("T", [P, TCOLS, P])
        across = [sb(f"across{n}", [P, P]) for n in range(2)]
        V = sb("V", [P, VN * H])
        w1 = sb("w1", [P, F * F])
        w1f = sb("w1f", [P, F * F])
        w2 = sb("w2", [P, F * H])
        vidx = sb("vidx", [P, 4], I32)
        scratch = sb("scratch", [P, 2 * VN * H])
        other = [[scratch[:, 2 * V0[c] * H + t * JN[c] * H:][:, 0:JN[c] * H] for t in range(2)] for c in range(2)]
        stage = [scratch[:, n * HALF * H:(n + 1) * HALF * H] for n in range(4)]
        zero = sb("zero", [F, H])
        small = {name: sb(f"s_{name}", shape) for name, shape in SMALL}
        cin_bk = sb("cin_bk", [P, 2])
        z = sb("z", [P, 2, P])
        h1 = sb("h1", [P, N1 // P, P])
        h2 = sb("h2", [P, N2 // P, P])
        y = sb("y", [1, B])

        def bank(name):
            return ctx.enter_context(nc.psum_tensor(name, [P, 512], F32))

        tps = [bank(f"tps{n}") for n in range(4)]
        zps = [bank(f"zps{n}") for n in range(2)]
        mps = [bank(f"mps{n}") for n in range(2)]

        udram = nc.dram_tensor("udram", [UROWS + 1, F * H], F32, kind="Internal").ap()

        idx_loaded = [sem(f"idx_loaded{n}") for n in range(2)]
        w12_loaded = sem("w12_loaded")
        small_loaded = sem("small_loaded")
        gather_begun = sem("gather_begun")
        vidx_loaded = sem("vidx_loaded")
        gathered = [sem(f"gathered{n}") for n in range(2)]
        emb_ready = [sem(f"emb_ready{n}") for n in range(2)]
        prod_ready = [sem(f"prod_ready{n}") for n in range(2)]
        mov_ready = [sem(f"mov_ready{n}") for n in range(2)]
        half_used = [sem(f"half_used{n}") for n in range(2)]
        tps_full = [sem(f"tps_full{n}") for n in range(4)]
        tps_free = [sem(f"tps_free{n}") for n in range(4)]
        zeroed = sem("zeroed")
        preset = sem("preset")
        w1f_ready = sem("w1f_ready")
        w1r_ready = sem("w1r_ready")
        zw_ready = sem("zw_ready")
        pre_full = sem("pre_full")
        pre_free = sem("pre_free")
        u_written = [sem(f"u_written{n}") for n in range(4)]
        uzero_written = sem("uzero_written")
        v_gathered = sem("v_gathered")
        v_step = sem("v_step")
        v_ready = sem("v_ready")
        across_ready = sem("across_ready")
        z_full = sem("z_full")
        z_ready = sem("z_ready")
        h_full = sem("h_full")
        h_ready = sem("h_ready")
        y_stored = sem("y_stored")

        block = ctx.enter_context(nc.Block())

        USTAGES = [(g, r, min(r + P, HALF * F)) for g in range(2) for r in range(0, HALF * F, P)]
        UQ = [(q, min(4, HALF - q)) for q in range(0, HALF, 4)]
        VSTEPS = [(c, j, min(4, JN[c] - j)) for c in range(2) for j in range(0, JN[c], 4)]
        PRE = len(USTAGES) * len(UQ) + len(VSTEPS)
        UPARTS = [[(r // F, max(r, r0), min(r + F, r1)) for r in range(r0 // F * F, r1, F)] for _, r0, r1 in USTAGES]
        WRITES = [sum(len(UPARTS[s]) for s in range(b, len(USTAGES), 4)) for b in range(4)]

        @block.sync
        def _(sp):
            sp.dma_start(idx[0][:], io["ids"][0:P, :]).then_inc(idx_loaded[0], 16)
            sp.dma_start(idx[1][:], io["ids"][P:2 * P, :]).then_inc(idx_loaded[1], 16)
            sp.dma_start(w1[:], io["w1"]).then_inc(w12_loaded, 16)
            sp.dma_start(w2[:], io["w2"]).then_inc(w12_loaded, 16)
            sp.dma_start(vidx[:], io["vidx"]).then_inc(vidx_loaded, 16)
            for name, _ in SMALL:
                sp.dma_start(small[name][:], io[name]).then_inc(small_loaded, 16)
            sp.wait_ge(zeroed, 1)
            sp.dma_start(udram[UROWS:UROWS + 1, :].rearrange("o (j h) -> (o j) h", h=H), zero[:]).then_inc(uzero_written, 16)
            for s, (g, r0, _) in enumerate(USTAGES):
                sp.wait_ge(pre_free, len(UQ) * (s + 1))
                for p, a, b in UPARTS[s]:
                    row, j = (g * HALF + p) * HALF, a - p * F
                    dst = udram[row:row + HALF, j * H:(j + b - a) * H].rearrange("q (j h) -> j q h", h=H)
                    src = stage[s % 4][a - r0:b - r0, :].rearrange("j (q h) -> j q h", h=H)
                    sp.dma_start(dst, src).then_inc(u_written[s % 4], 16)

            def spread(it, par):
                for bk in (0, 2):
                    sp.wait_ge(tps_free[bk], 4 * (2 * it + par) + 5)
                for part, (q0, q1) in enumerate(XQ):
                    for q in range(q0, q1):
                        sp.dma_start(across[part][(q - q0) * HALF:(q - q0 + 1) * HALF, :],
                                     T[0:HALF, TJ[0] + HALF - J0[0] + q, :]).then_inc(across_ready, 16)

            with sp.Fori(0, TILES // 2 - 1) as it:
                for par in range(2):
                    sp.wait_ge(gathered[par], it * (16 * F) + 16 * F)
                    sp.dma_start(idx[par][:], io["ids"][bass.ds(it * (2 * P) + (2 + par) * P, P), :]
                                 ).then_inc(idx_loaded[par], 16)
                    spread(it, par)
            for par in range(2):
                spread(TILES // 2 - 1, par)

        @block.gpsimd
        def _(pool):
            def gather_tile(it, par):
                pool.wait_ge(idx_loaded[par], 16 * (it + 1))
                pool.wait_ge(emb_ready[par], it + 1)
                pool.sem_inc(gather_begun, 1)
                for f in range(F):
                    nc.gpsimd.indirect_dma_start(
                        out=rows[par][:, f * K:(f + 1) * K], out_offset=None, in_=tables[f],
                        in_offset=bass.IndirectOffsetOnAxis(ap=idx[par][:, f:f + 1], axis=0),
                    ).then_inc(gathered[par], 16)

            gather_tile(0, 0)
            pool.wait_ge(vidx_loaded, 16)
            pool.wait_ge(uzero_written, 16)
            for b in range(4):
                pool.wait_ge(u_written[b], 16 * WRITES[b])
            for c in range(2):
                for t in range(2):
                    nc.gpsimd.indirect_dma_start(
                        out=other[c][t][0:RN[c], :], out_offset=None, in_=udram,
                        in_offset=bass.IndirectOffsetOnAxis(ap=vidx[0:RN[c], 2 * c + t:2 * c + t + 1], axis=0),
                        element_offset=J0[c] * H,
                    ).then_inc(v_gathered, 16)
            gather_tile(0, 1)
            with pool.Fori(1, TILES // 2) as it:
                for par in range(2):
                    gather_tile(it, par)

        @block.vector
        def _(dve):
            for par in range(2):
                dve.sem_inc(emb_ready[par], 1)
            nc.vector.memset(zero[:], 0.0).then_inc(zeroed, 1)
            for n in range(2):
                last = nc.vector.memset(mov[n][:], 0.0)
            last.then_inc(zeroed, 1)
            dve.wait_ge(zeroed, 2)
            for n in range(2):
                for g in range(FOUR):
                    for col in (0, MCOLS - 1):
                        nc.vector.memset(mov[n][g * K:(g + 1) * K, :, g, col:col + 1], 1.0)
                last = nc.vector.memset(prod[n][:, :, ONE_ROW:ONE_ROW + 1], 1.0)
            last.then_inc(preset, 1)
            dve.wait_ge(w12_loaded, 32)
            a = w1[:].rearrange("i (p q) -> i p q", q=F)
            nc.vector.tensor_tensor(w1f[:].rearrange("i (p q) -> i p q", q=F), a, w1[:].rearrange("i (q p) -> i p q", p=F),
                                    ALU.add).then_inc(w1f_ready, 1)
            dve.wait_ge(small_loaded, 16 * len(SMALL))
            nc.vector.tensor_tensor(small["w1a"][:], small["w1a"][:], small["w1b"][:], ALU.add).then_inc(w1r_ready, 1)
            nc.vector.tensor_tensor(small["z1a"][:], small["z1a"][:], small["z1b"][:], ALU.add).then_inc(zw_ready, 1)
            dve.wait_ge(zw_ready, 1)
            for c in range(2):
                part = small["z1a"][:, c * H:(c + 1) * H]
                nc.vector.tensor_scalar(part, part, small["zmult"][:, c:c + 1], None, ALU.mult)
            nc.vector.tensor_tensor(small["xa"][:], small["xa"][:], small["xb"][:], ALU.add)
            nc.vector.tensor_scalar(cin_bk[:], small["cin_b"][:], float(K), None, ALU.mult).then_inc(zw_ready, 1)

            def tile(it, par):
                n = 2 * it + par
                dve.wait_ge(gathered[par], (it + 1) * (16 * F))
                nc.vector.transpose(emb[par][:].rearrange("p u f -> p f u"),
                                    rows[par][:].rearrange("p (f k) -> p f k", k=K)).then_inc(emb_ready[par], 1)
                for h in range(2):
                    if h == 0:
                        dve.wait_ge(emb_ready[par], it + 2)
                    dve.wait_ge(half_used[h], n + 1)
                    e = emb[par][:, h * U_HALF:(h + 1) * U_HALF, :]
                    q = prod[h]

                    def rectangle(row, p0, np_, q0, nq):
                        shape = [P, U_HALF, np_, nq]
                        return nc.vector.tensor_tensor(
                            q[:, :, row:row + np_ * nq].rearrange("p u (a b) -> p u a b", b=nq),
                            e[:, :, p0:p0 + np_].unsqueeze(3).to_broadcast(shape),
                            e[:, :, q0:q0 + nq].unsqueeze(2).to_broadcast(shape), ALU.mult)

                    def triangle(row, p0, np_):
                        for p in range(np_ - 1):
                            w = np_ - 1 - p
                            nc.vector.tensor_tensor(
                                q[:, :, row:row + w], e[:, :, p0 + p:p0 + p + 1].to_broadcast([P, U_HALF, w]),
                                e[:, :, p0 + p + 1:p0 + np_], ALU.mult)
                            row += w

                    row = HALF
                    nc.vector.tensor_copy(q[:, :, 0:HALF], e[:, :, 0:HALF])
                    rectangle(row, 0, 5, 5, 8)
                    rectangle(row + 40, 5, 5, 10, 3)
                    triangle(row + 55, 10, 3)
                    row = R0[1]
                    nc.vector.tensor_tensor(q[:, :, row:row + F], e, e, ALU.mult)
                    row += F
                    for p0, np_ in ((0, 5), (5, 5), (19, 4), (23, 3)):
                        triangle(row, p0, np_)
                        row += np_ * (np_ - 1) // 2
                    row += 1
                    rectangle(row, 13, 6, 19, 7)
                    triangle(row + 42, 13, 6)
                    rectangle(row + 57, 19, 4, 23, 3).then_inc(prod_ready[h], 1)

            tile(0, 0)
            dve.wait_ge(v_gathered, 64)
            dve.wait_ge(pre_free, PRE)
            step = 0
            for c in range(2):
                n = RN[c]
                x, v = other[c][0][0:n, :], V[0:n, V0[c] * H:(V0[c] + JN[c]) * H]
                m = small["mult"][0:n, V0[c]:V0[c] + JN[c]].unsqueeze(2).to_broadcast([n, JN[c], H])
                v3 = v.rearrange("r (j h) -> r j h", h=H)
                nc.vector.tensor_tensor(x, x, other[c][1][0:n, :], ALU.add).then_inc(v_step, 1)
                dve.wait_ge(v_step, step + 1)
                nc.vector.tensor_tensor(v, v, x, ALU.add).then_inc(v_step, 1)
                dve.wait_ge(v_step, step + 2)
                nc.vector.tensor_tensor(v3, v3, m, ALU.mult).then_inc(v_ready, 1)
                step += 2
            tile(0, 1)
            with dve.Fori(1, TILES // 2) as it:
                for par in range(2):
                    tile(it, par)

        @block.scalar
        def _(act):
            n = 0
            for s, (g, r0, r1) in enumerate(USTAGES):
                if s >= 4:
                    act.wait_ge(u_written[s % 4], 16 * len(UPARTS[s - 4]))
                for q, nq in UQ:
                    act.wait_ge(pre_full, n + 1)
                    nc.scalar.copy(stage[s % 4][0:r1 - r0, q * H:(q + nq) * H],
                                   tps[n % 4][0:r1 - r0, 0:nq * H]).then_inc(pre_free, 1)
                    n += 1
            for c, j, nj in VSTEPS:
                act.wait_ge(pre_full, n + 1)
                nc.scalar.copy(V[0:RN[c], (V0[c] + j) * H:(V0[c] + j + nj) * H],
                               tps[n % 4][0:RN[c], 0:nj * H]).then_inc(pre_free, 1)
                n += 1
            for bk in range(4):
                act.sem_inc(tps_free[bk], 1)
            act.wait_ge(preset, 1)
            act.wait_ge(zw_ready, 2)

            def fill_mov(it, par):
                for h in range(2):
                    act.wait_ge(emb_ready[par], it + 2)
                    act.wait_ge(half_used[h], 2 * it + (par + 1))
                    for g in range(FOUR):
                        last = nc.scalar.copy(mov[h][g * K:(g + 1) * K, :, g, 1:1 + F],
                                              emb[par][g * K:(g + 1) * K, h * U_HALF:(h + 1) * U_HALF, :])
                    last.then_inc(mov_ready[h], 1)

            def take_t(n):
                for k in range(16):
                    c, u0, bk = k % 2, k // 2 * EVAC, k % 4
                    if k % 8 == 7:
                        act.wait_ge(half_used[k // 8], n + 2)
                    elif bk == 3:
                        act.wait_ge(tps_full[bk], 2 * n + (k // 8 + 1))
                    else:
                        act.wait_ge(tps_full[bk], 4 * n + (k // 4 + 1))
                    src = tps[bk][0:RN[c], 0:EVAC * FOUR * CN[c]].rearrange("r (u g c) -> r c g u", g=FOUR, c=CN[c])
                    dst = T[0:RN[c], T0[c]:T0[c] + CN[c], :].rearrange("r c (g u) -> r c g u", g=FOUR)
                    nc.scalar.copy(dst[:, :, :, u0:u0 + EVAC], src).then_inc(tps_free[bk], 1)

            def take_z(n):
                for s in (1, 0):
                    act.wait_ge(z_full, 2 * n + (2 - s))
                    nc.scalar.activation(z[:, s, :], zps[s][:, 0:P], ACT.Identity,
                                         bias=cin_bk[:, s:s + 1]).then_inc(z_ready, 1)

            def take_mlp(n):
                for s in range(7):
                    act.wait_ge(h_full, 7 * n + (s + 1))
                    src = mps[s % 2]
                    if s < 4:
                        nc.scalar.activation(h1[:, s, :], src[:, 0:P], ACT.Relu,
                                             bias=small["b_top1"][:, s:s + 1]).then_inc(h_ready, 1)
                    elif s < 6:
                        nc.scalar.activation(h2[:, s - 4, :], src[:, 0:P], ACT.Relu,
                                             bias=small["b_top2"][:, s - 4:s - 3]).then_inc(h_ready, 1)
                    else:
                        nc.scalar.copy(y[:, bass.ds(n * P, P)], src[0:1, 0:P]).then_inc(h_ready, 1)

            fill_mov(0, 0)
            take_t(0)
            fill_mov(0, 1)
            take_z(0)
            with act.Fori(0, TILES // 2 - 1) as it:
                take_t(2 * it + 1)
                take_mlp(2 * it)
                fill_mov(it + 1, 0)
                take_z(2 * it + 1)
                take_t(2 * it + 2)
                take_mlp(2 * it + 1)
                fill_mov(it + 1, 1)
                take_z(2 * it + 2)
            take_t(TILES - 1)
            take_mlp(TILES - 2)
            take_z(TILES - 1)
            take_mlp(TILES - 1)
            act.wait_ge(h_ready, 7 * TILES)
            act.dma_start(out.rearrange("b o -> o b"), y[:]).then_inc(y_stored, 16)
            act.wait_ge(y_stored, 16)

        @block.tensor
        def _(pe):
            pe.wait_ge(w12_loaded, 32)
            for h in range(2):
                pe.sem_inc(half_used[h], 1)
            pe.wait_ge(w1f_ready, 1)
            n = 0
            for g, r0, r1 in USTAGES:
                for q, nq in UQ:
                    if n >= 4:
                        pe.wait_ge(pre_free, n - 3)
                    first = (g * HALF + q) * H
                    nc.tensor.matmul(tps[n % 4][0:r1 - r0, 0:nq * H], w1f[:, g * HALF * F + r0:g * HALF * F + r1],
                                     w2[:, first:first + nq * H], start=True, stop=True).then_inc(pre_full, 1)
                    n += 1
            pe.wait_ge(w1r_ready, 1)
            for c, j, nj in VSTEPS:
                pe.wait_ge(pre_free, n - 3)
                nc.tensor.matmul(tps[n % 4][0:RN[c], 0:nj * H], small["w1a"][:, c * P:c * P + RN[c]],
                                 w2[:, (J0[c] + j) * H:(J0[c] + j + nj) * H], start=True, stop=True).then_inc(pre_full, 1)
                n += 1
            pe.wait_ge(pre_free, PRE)
            pe.wait_ge(zw_ready, 2)

            def make_t(n):
                for h in range(2):
                    pe.wait_ge(mov_ready[h], n + 1)
                    pe.wait_ge(prod_ready[h], n + 1)
                    for k in range(8 * h, 8 * h + 8):
                        c, bk = k % 2, k % 4
                        pe.wait_ge(tps_free[bk], 4 * n + (k // 4 + 1))
                        w = FOUR * CN[c]
                        for v in range(EVAC):
                            u = k // 2 * EVAC + v - h * U_HALF
                            last = nc.tensor.matmul(
                                tps[bk][0:RN[c], v * w:(v + 1) * w], prod[h][:, u, R0[c]:R0[c] + RN[c]],
                                mov[h][:, u, :, C0[c]:C0[c] + CN[c]], start=True, stop=True)
                        last.then_inc(half_used[h] if k % 8 == 7 else tps_full[bk], 1)

            def make_z(n):
                for bk in range(4):
                    pe.wait_ge(tps_free[bk], 4 * n + 5)
                for c in range(2):
                    for j in range(JN[c]):
                        v = (V0[c] + j) * H
                        last = nc.tensor.matmul(zps[1][:, 0:P], V[0:RN[c], v:v + H], T[0:RN[c], TJ[c] + j, :],
                                                start=(c == 0 and j == 0), stop=(c == 1 and j == JN[1] - 1))
                last.then_inc(z_full, 1)
                for c in range(2):
                    nc.tensor.matmul(zps[0][:, 0:P], small["z1a"][0:RN[c], c * H:(c + 1) * H],
                                     T[0:RN[c], TONE[c], :], start=(c == 0), stop=False)
                pe.wait_ge(across_ready, n * (16 * HALF) + 16 * HALF)
                for part, (q0, q1) in enumerate(XQ):
                    m = (q1 - q0) * HALF
                    last = nc.tensor.matmul(zps[0][:, 0:P], small["xa"][0:m, part * H:(part + 1) * H],
                                            across[part][0:m, :], start=False, stop=(part == 1))
                last.then_inc(z_full, 1)

            def mlp(n):
                for s in range(7):
                    if s == 0:
                        pe.wait_ge(z_ready, 2 * n + 2)
                    elif s >= 2:
                        pe.wait_ge(h_ready, 7 * n + (4 if s == 4 else 6 if s == 6 else s - 1))
                    if s < 4:
                        for k in range(2):
                            nc.tensor.matmul(mps[s % 2][:, 0:P], small["top1"][:, k * N1 + s * P:k * N1 + (s + 1) * P],
                                             z[:, k, :], start=(k == 0), stop=False)
                        last = nc.tensor.matmul(mps[s % 2][:, 0:P], small["top1d"][:, s * P:(s + 1) * P],
                                                small["dense"][:, bass.ds(n * P, P)], start=False, stop=True)
                    elif s < 6:
                        for k in range(4):
                            w = k * N2 + (s - 4) * P
                            last = nc.tensor.matmul(mps[s % 2][:, 0:P], small["top2"][:, w:w + P], h1[:, k, :],
                                                    start=(k == 0), stop=(k == 3))
                    else:
                        for k in range(2):
                            last = nc.tensor.matmul(mps[s % 2][0:1, 0:P], small["top3"][:, k:k + 1], h2[:, k, :],
                                                    start=(k == 0), stop=(k == 1))
                    last.then_inc(h_full, 1)

            make_t(0)
            pe.wait_ge(v_ready, 2)
            make_z(0)
            with pe.Fori(0, TILES // 2 - 1) as it:
                for par in range(2):
                    make_t(2 * it + (par + 1))
                    mlp(2 * it + par)
                    make_z(2 * it + (par + 1))
            make_t(TILES - 1)
            mlp(TILES - 2)
            make_z(TILES - 1)
            mlp(TILES - 1)


def by_rows(first, second):
    idx = np.zeros((2, 2, P), np.int64)
    is_pair = np.zeros((2, P), bool)
    for c in range(2):
        for r, row in enumerate(ROWS[R0[c]:R0[c] + RN[c]]):
            if row != "one" and row[0] != "single":
                idx[0, c, r], idx[1, c, r] = row
                is_pair[c, r] = True
    return idx[first], idx[second], is_pair


def kernel(**inputs):
    import concourse.bacc as bacc
    from concourse.bass_utils import run_bass_kernel_spmd

    a = {k: np.asarray(v) for k, v in inputs.items()}
    W1, W2 = a["L0_rec_W1"], a["L0_rec_W2"]
    mult, zmult, index = plan()
    one = np.array([[r < RN[c] and ROWS[R0[c] + r] == "one" for r in range(P)] for c in range(2)])
    arrays = {"ids": a["ids"], "w1": W1.reshape(H, F * F), "w2": W2.transpose(1, 2, 0).reshape(H, F * H),
              "mult": mult, "zmult": zmult, "vidx": index}
    for name, order in (("a", (0, 1)), ("b", (1, 0))):
        p, q, is_pair = by_rows(*order)
        rows = np.where(is_pair[None], W1[:, p, q], np.float32(0))
        arrays["z1" + name] = rows.transpose(2, 1, 0).reshape(P, 2 * H)
        if name == "a":
            rows = np.where(one[None], a["L0_rec_b1"][:, None, None], rows)
        arrays["w1" + name] = rows.reshape(H, 2 * P)
    for name, rows in (("xa", W1[:, :HALF, HALF:].transpose(2, 1, 0)), ("xb", W1[:, HALF:, :HALF].transpose(1, 2, 0))):
        x = np.zeros((P, 2, H), W1.dtype)
        for part, (q0, q1) in enumerate(XQ):
            x[:(q1 - q0) * HALF, part] = rows[q0:q1].reshape(-1, H)
        arrays[name] = x.reshape(P, 2 * H)
    arrays["cin_b"] = np.stack([a["L0_rec_b1"], a["L0_rec_b2"]], axis=1)
    arrays["b_top1"] = a["b_top1"].reshape(N1 // P, P).T
    arrays["b_top2"] = a["b_top2"].reshape(N2 // P, P).T
    arrays["top1"] = a["W_top1"][:2 * H].reshape(2, P, N1).transpose(1, 0, 2).reshape(P, 2 * N1)
    arrays["top1d"] = a["W_top1"][2 * H:]
    arrays["top2"] = a["W_top2"].reshape(N1 // P, P, N2).transpose(1, 0, 2).reshape(P, -1)
    arrays["top3"] = a["W_top3"].reshape(N2 // P, P).T
    arrays["dense"] = a["dense_ctx"].T
    for f in range(F):
        arrays[f"tbl_{f}"] = a[f"tbl_{f}"]

    nc = bacc.Bacc("TRN2", target_bir_lowering=False, num_devices=1)
    maps, aps = {}, {}
    for name, x in arrays.items():
        x = np.ascontiguousarray(x)
        maps["in_" + name] = x
        aps[name] = nc.dram_tensor("in_" + name, x.shape, mybir.dt.from_np(x.dtype), kind="ExternalInput").ap()
    out = nc.dram_tensor("out", (B, 1), F32, kind="ExternalOutput").ap()
    build(nc, aps, [aps[f"tbl_{f}"] for f in range(F)], out)
    r = run_bass_kernel_spmd(nc, [maps], core_ids=[0])
    return r.results[0]["out"]
```

```python
from contextlib import ExitStack

import numpy as np

import concourse.bass as bass
from concourse import mybir

F32 = mybir.dt.float32
BF16 = mybir.dt.bfloat16
I32 = mybir.dt.int32
ALU = mybir.AluOpType
ACT = mybir.ActivationFunctionType

P = 128
B = 1024
F = 26
HALF = F // 2
K = 32
H = 128
D = 16
N1, N2 = 512, 256
GROUPS = ((0, HALF), (HALF, 19), (19, 23), (23, F))
PICKED = (6,)
GATHERED = [[f for f in range(f0, f1) if f not in PICKED] for f0, f1 in GROUPS]
SLICES = 8
BEFORE_V = 2
PICK_AT = 7
TOP3_AT = 3
Z1_AT = 12
TILES = B // P
U_HALF = 16
FOUR = 4
EVAC = 4
HOT_AT = (1, P)
HOT0 = 256

MCOLS = F + 2


def tri(fields):
    fields = list(fields)
    return [(p, q) for n, p in enumerate(fields) for q in fields[n + 1:]]


def rect(first, second):
    return [(p, q) for p in first for q in second]


PART_A = [("single", f) for f in range(HALF)] + rect(range(0, 5), range(5, 13)) + rect(range(5, 10), range(10, 13)) \
    + tri(range(10, 13))
PART_S = [(f, f) for f in range(F)] + tri(range(0, 5)) + tri(range(5, 10)) + tri(range(19, 23)) \
    + tri(range(23, 26)) + ["one"]
PART_B = rect(range(13, 19), range(19, 26)) + tri(range(13, 19)) + rect(range(19, 23), range(23, 26))
ROWS = PART_A + PART_S + PART_B
R0 = (0, len(PART_A) - 1)
RN = (len(PART_A) + len(PART_S), 1 + len(PART_S) + len(PART_B))
ONE_ROW = len(PART_A) + len(PART_S) - 1
J0 = (10, 0)
JN = (16, 19)
C0 = (J0[0] + 1, 0)
PAIRED = ((13, 14), (15, 16), (17, 18))
LOW = 64
ALONE = JN[1] - 2 * len(PAIRED)
CN = (JN[0] + 1, ALONE + 1)
T0 = (0, CN[0])
TPAIR = CN[0] + CN[1]
TCOLS = TPAIR + len(PAIRED)
TJ = (0, CN[0] + 1)
TONE = (JN[0], CN[0])
VN = sum(JN)
V0 = (0, JN[0])
Z2 = [[(j, TJ[c] + j) for j in range(n)] for c, n in enumerate((JN[0], ALONE))]
Z2[1] += [(upper, TPAIR + n) for n, (_, upper) in enumerate(PAIRED)]
UROWS = 2 * HALF * HALF


XQ = ((0, 9), (9, HALF))


def plan():
    mult = np.zeros((P, VN), np.float32)
    zmult = np.zeros((P, 2), np.float32)
    index = np.full((P, 4), UROWS, np.int32)
    seen, pairs, ones = set(), set(), set()
    for c in range(2):
        for r in reversed(range(RN[c])):
            row = ROWS[R0[c] + r]
            for j in range(J0[c], J0[c] + JN[c]):
                if row == "one":
                    if j not in ones:
                        ones.add(j)
                        mult[r, V0[c] + j - J0[c]] = 1.0
                elif row[0] != "single":
                    key = tuple(sorted(row + (j,)))
                    if key not in seen:
                        seen.add(key)
                        mult[r, V0[c] + j - J0[c]] = (1.0, 0.5, 1.0 / 6.0)[3 - len(set(key))]
            if row != "one" and row[0] != "single":
                p, q = row
                index[r, 2 * c] = p * HALF + q % HALF
                index[r, 2 * c + 1] = q * HALF + p % HALF
                if row not in pairs:
                    pairs.add(row)
                    zmult[r, c] = 0.5 if p == q else 1.0
    assert len(seen) == F * (F + 1) * (F + 2) // 6 and len(ones) == F
    assert len(pairs) == 2 * (HALF * (HALF + 1) // 2)
    assert not mult[:LOW, V0[1] + PAIRED[0][0]:].any() and RN[1] - LOW <= LOW
    assert not zmult[:(XQ[1][1] - XQ[1][0]) * HALF, 1].any()
    return mult, zmult, index


PARTS = (("h", "h"), ("h", "m"), ("m", "h"), ("m", "m"), ("h", "l"), ("l", "h"), ("m", "l"), ("l", "m"))

SMALL = [
    ("w1a", [P, 2 * P]), ("w1b", [P, 2 * P]), ("mult", [P, VN]), ("zmult", [P, 2]), ("z1a", [P, 2 * H]),
    ("z1b", [P, 2 * H]), ("xa", [P, 2 * H]), ("xb", [P, 2 * H]), ("cin_b", [P, 2]),
    ("minus", [P, 4]),
]
TOP = [
    ("b_top1", [P, N1 // P]), ("b_top2", [P, N2 // P]), ("top1", [P, 2 * N1]), ("top2", [P, N1 // P * N2]),
    ("top3", [P, N2 // P]),
]


def build(nc, io, tables, out):
    with ExitStack() as ctx:
        def sb(name, shape, dt=F32):
            return ctx.enter_context(nc.sbuf_tensor(name, shape, dt))

        def sem(name):
            return ctx.enter_context(nc.semaphore(name))

        idx = [sb(f"idx{n}", [P, F], I32) for n in range(2)]
        rows = [sb(f"rows{n}", [P, F * K]) for n in range(2)]
        emb = [sb(f"emb{n}", [P, 2 * U_HALF, F]) for n in range(2)]
        mov = [sb(f"mov{n}", [P, U_HALF, FOUR, MCOLS]) for n in range(2)]
        prod = [sb(f"prod{n}", [P, U_HALF, len(ROWS)]) for n in range(2)]
        T = [sb(f"T{n}", [P, TCOLS, P]) for n in range(2)]
        across = sb("across", [P, P])
        V = sb("V", [P, VN * H])
        w1 = sb("w1", [P, F * F])
        w1f = sb("w1f", [P, F * F])
        w2 = sb("w2", [P, F * H])
        vidx = sb("vidx", [P, 4], I32)
        picked = []
        for f in PICKED:
            vp = tables[f].shape[0] // SLICES
            assert vp * SLICES == tables[f].shape[0] and vp <= P
            picked.append((f, vp, sb(f"table{f}", [vp, SLICES, K]), sb(f"parts{f}", [vp, SLICES, 3, K], BF16),
                           sb(f"ids{f}", [vp, B], I32), sb(f"hot{f}", [vp, SLICES, P], BF16)))
        numbers = sb("numbers", [P, SLICES], I32)
        scratch = sb("scratch", [P, 2 * VN * H])
        other = [[scratch[:, 2 * V0[c] * H + t * JN[c] * H:][:, 0:JN[c] * H] for t in range(2)] for c in range(2)]
        stage = [scratch[:, n * HALF * H:(n + 1) * HALF * H] for n in range(4)]
        zero = sb("zero", [F, H])
        small = {name: sb(f"s_{name}", shape) for name, shape in SMALL + TOP}
        dense = [sb("dense", [P, B]), sb("top1d", [P, N1])]
        high = [sb("dense_high", [P, B], BF16), sb("top1d_high", [P, N1], BF16)]
        part = [sb("dense_part", [P, B], BF16), sb("top1d_part", [P, N1], BF16)]
        cin_bk = sb("cin_bk", [P, 2])
        z = sb("z", [P, 2, P])
        h1 = sb("h1", [P, N1 // P, P])
        h2 = sb("h2", [P, N2 // P, P])
        y = sb("y", [1, B])

        def bank(name):
            return ctx.enter_context(nc.psum_tensor(name, [P, 512], F32))

        tps = [bank(f"tps{n}") for n in range(4)]
        zps = [bank(f"zps{n}") for n in range(2)]
        mps = [bank(f"mps{n}") for n in range(2)]

        udram = nc.dram_tensor("udram", [UROWS + 1, F * H], F32, kind="Internal").ap()
        cross = nc.dram_tensor("cross", [HALF * HALF, P], F32, kind="Internal").ap()

        table_loaded = sem("table_loaded")
        ids_loaded = [sem(f"ids_loaded{n}") for n in range(2)]
        table_step = sem("table_step")
        hot_ready = sem("hot_ready")
        hot_full = sem("hot_full")
        hot_rows = sem("hot_rows")
        idx_loaded = [sem(f"idx_loaded{n}") for n in range(2)]
        w1_loaded = sem("w1_loaded")
        w2_loaded = [sem(f"w2_loaded{n}") for n in range(2)]
        small_loaded = sem("small_loaded")
        top_loaded = sem("top_loaded")
        dense_loaded = sem("dense_loaded")
        split_step = sem("split_step")
        dense_ready = sem("dense_ready")
        gather_begun = sem("gather_begun")
        vidx_loaded = sem("vidx_loaded")
        gathered = [[sem(f"gathered{n}_{g}") for g in range(len(GROUPS))] for n in range(2)]
        turned = [[sem(f"turned{n}_{g}") for g in range(len(GROUPS) - 1)] for n in range(2)]
        emb_ready = [sem(f"emb_ready{n}") for n in range(2)]
        prod_ready = [sem(f"prod_ready{n}") for n in range(2)]
        mov_ready = [sem(f"mov_ready{n}") for n in range(2)]
        half_used = [sem(f"half_used{n}") for n in range(2)]
        tps_full = [sem(f"tps_full{n}") for n in range(4)]
        tps_free = [sem(f"tps_free{n}") for n in range(4)]
        zeroed = sem("zeroed")
        preset = sem("preset")
        w1f_ready = sem("w1f_ready")
        w1r_ready = sem("w1r_ready")
        zw_ready = sem("zw_ready")
        pre_full = sem("pre_full")
        pre_free = sem("pre_free")
        u_written = [sem(f"u_written{n}") for n in range(4)]
        uzero_written = sem("uzero_written")
        v_gathered = [[sem(f"v_gathered{n}_{t}") for t in range(2)] for n in range(2)]
        v_step = sem("v_step")
        v_ready = sem("v_ready")
        cross_written = sem("cross_written")
        across_ready = sem("across_ready")
        z_full = sem("z_full")
        z_ready = sem("z_ready")
        h_full = sem("h_full")
        h_ready = sem("h_ready")
        y_stored = sem("y_stored")

        block = ctx.enter_context(nc.Block())

        USTAGES = [(g, r, min(r + P, HALF * F)) for g in range(2) for r in range(0, HALF * F, P)]
        UQ = [(q, min(4, HALF - q)) for q in range(0, HALF, 4)]
        VSTEPS = [(c, j, min(4, JN[c] - j)) for c in range(2) for j in range(0, JN[c], 4)]
        PRE = len(USTAGES) * len(UQ) + len(VSTEPS)
        UPARTS = [[(r // F, max(r, r0), min(r + F, r1)) for r in range(r0 // F * F, r1, F)] for _, r0, r1 in USTAGES]
        WRITES = [sum(len(UPARTS[s]) for s in range(b, len(USTAGES), 4)) for b in range(4)]

        @block.sync
        def _(sp):
            sp.dma_start(idx[0][:], io["ids"][0:P, :]).then_inc(idx_loaded[0], 16)
            sp.dma_start(w1[:], io["w1"]).then_inc(w1_loaded, 16)
            for g in range(2):
                cols = slice(g * HALF * H, (g + 1) * HALF * H)
                sp.dma_start(w2[:, cols], io["w2"][:, cols]).then_inc(w2_loaded[g], 16)
            sp.dma_start(idx[1][:], io["ids"][P:2 * P, :]).then_inc(idx_loaded[1], 16)
            sp.dma_start(vidx[:], io["vidx"]).then_inc(vidx_loaded, 16)
            for name, _ in SMALL:
                sp.dma_start(small[name][:], io[name]).then_inc(small_loaded, 16)
            sp.dma_start(numbers[:], io["numbers"]).then_inc(table_loaded, 16)
            for f, vp, table, _, ids, _ in picked:
                sp.dma_start(table[:], tables[f].rearrange("(p s) k -> p s k", s=SLICES)).then_inc(table_loaded, 16)
                sp.dma_start(ids[:, 0:2 * P], io[f"ids{f}"][:, 0:2 * P].to_broadcast([vp, 2 * P])
                             ).then_inc(ids_loaded[0], 16)
            for x, name in zip(dense, ("dense", "top1d")):
                sp.dma_start(x[:], io[name]).then_inc(dense_loaded, 16)
            sp.wait_ge(zeroed, 1)
            sp.dma_start(udram[UROWS:UROWS + 1, :].rearrange("o (j h) -> (o j) h", h=H), zero[:]
                         ).then_inc(uzero_written, 16)
            for s, (g, r0, _) in enumerate(USTAGES):
                sp.wait_ge(pre_free, len(UQ) * (s + 1))
                for p, a, b in UPARTS[s]:
                    row, j = (g * HALF + p) * HALF, a - p * F
                    dst = udram[row:row + HALF, j * H:(j + b - a) * H].rearrange("q (j h) -> j q h", h=H)
                    src = stage[s % 4][a - r0:b - r0, :].rearrange("j (q h) -> j q h", h=H)
                    sp.dma_start(dst, src).then_inc(u_written[s % 4], 16)

            for f, vp, _, _, ids, _ in picked:
                sp.dma_start(ids[:, 2 * P:], io[f"ids{f}"][:, 2 * P:].to_broadcast([vp, B - 2 * P])
                             ).then_inc(ids_loaded[1], 16)
            for name, _ in TOP:
                sp.dma_start(small[name][:], io[name]).then_inc(top_loaded, 16)

            def spread(it, par):
                for bk in range(4):
                    sp.wait_ge(tps_free[bk], 4 * (2 * it + par) + 5)
                first = TJ[0] + HALF - J0[0]
                sp.dma_start(cross.rearrange("(q p) b -> p q b", p=HALF),
                             T[par][0:HALF, first:first + HALF, :]).then_inc(cross_written, 16)
                sp.wait_ge(cross_written, 16 * (2 * it + par) + 16)
                for (q0, q1), to in zip(XQ, (across, T[par][:, TONE[1], :])):
                    sp.dma_start(to[0:(q1 - q0) * HALF, :], cross[q0 * HALF:q1 * HALF, :]).then_inc(across_ready, 16)

            with sp.Fori(0, TILES // 2 - 1) as it:
                for par in range(2):
                    for g, fields in enumerate(GATHERED):
                        sp.wait_ge(gathered[par][g], it * (16 * len(fields)) + 16 * len(fields))
                    sp.dma_start(idx[par][:], io["ids"][bass.ds(it * (2 * P) + (2 + par) * P, P), :]
                                 ).then_inc(idx_loaded[par], 16)
                    spread(it, par)
            for par in range(2):
                spread(TILES // 2 - 1, par)

        @block.gpsimd
        def _(pool):
            in_order = sum(GATHERED, [])

            def gather_fields(par, fields):
                for f in fields:
                    group = [f in g for g in GATHERED].index(True)
                    nc.gpsimd.indirect_dma_start(
                        out=rows[par][:, f * K:(f + 1) * K], out_offset=None, in_=tables[f],
                        in_offset=bass.IndirectOffsetOnAxis(ap=idx[par][:, f:f + 1], axis=0),
                    ).then_inc(gathered[par][group], 16)

            def gather_tile(it, par):
                pool.wait_ge(idx_loaded[par], 16 * (it + 1))
                pool.wait_ge(emb_ready[par], it + 1)
                pool.sem_inc(gather_begun, 1)
                gather_fields(par, in_order)

            gather_tile(0, 0)
            pool.wait_ge(idx_loaded[1], 16)
            gather_fields(1, in_order[:BEFORE_V])
            pool.wait_ge(vidx_loaded, 16)
            pool.wait_ge(uzero_written, 16)
            for b in range(4):
                pool.wait_ge(u_written[b], 16 * WRITES[b])
            for c in range(2):
                for t in range(2):
                    nc.gpsimd.indirect_dma_start(
                        out=other[c][t][0:RN[c], :], out_offset=None, in_=udram,
                        in_offset=bass.IndirectOffsetOnAxis(ap=vidx[0:RN[c], 2 * c + t:2 * c + t + 1], axis=0),
                        element_offset=J0[c] * H,
                    ).then_inc(v_gathered[c][t], 16)
            gather_fields(1, in_order[BEFORE_V:])
            with pool.Fori(1, TILES // 2) as it:
                for par in range(2):
                    gather_tile(it, par)

        @block.vector
        def _(dve):
            for par in range(2):
                dve.sem_inc(emb_ready[par], 1)
            nc.vector.memset(zero[:], 0.0).then_inc(zeroed, 1)
            for n in range(2):
                last = nc.vector.memset(mov[n][:], 0.0)
            last.then_inc(zeroed, 1)
            dve.wait_ge(zeroed, 2)
            for n in range(2):
                for g in range(FOUR):
                    for col in (0, MCOLS - 1):
                        nc.vector.memset(mov[n][g * K:(g + 1) * K, :, g, col:col + 1], 1.0)
                nc.vector.memset(T[n][LOW // 2:LOW, TPAIR:, :], 0.0)
                last = nc.vector.memset(prod[n][:, :, ONE_ROW:ONE_ROW + 1], 1.0)
            last.then_inc(preset, 1)
            dve.wait_ge(w1_loaded, 16)
            both = w1f[:].rearrange("i (p q) -> i p q", q=F)
            nc.vector.tensor_tensor(both, w1[:].rearrange("i (p q) -> i p q", q=F),
                                    w1[:].rearrange("i (q p) -> i p q", p=F), ALU.add).then_inc(w1f_ready, 1)
            dve.wait_ge(small_loaded, 16 * len(SMALL))
            nc.vector.tensor_tensor(small["w1a"][:], small["w1a"][:], small["w1b"][:], ALU.add).then_inc(w1r_ready, 1)
            nc.vector.tensor_tensor(small["z1a"][:], small["z1a"][:], small["z1b"][:], ALU.add).then_inc(zw_ready, 1)
            dve.wait_ge(zw_ready, 1)
            for c in range(2):
                half = small["z1a"][:, c * H:(c + 1) * H]
                nc.vector.tensor_scalar(half, half, small["zmult"][:, c:c + 1], None, ALU.mult)
            nc.vector.tensor_tensor(small["xa"][:], small["xa"][:], small["xb"][:], ALU.add).then_inc(zw_ready, 1)
            dve.wait_ge(zw_ready, 2)
            nc.vector.tensor_tensor(small["z1a"][:, H:], small["z1a"][:, H:], small["xa"][:, H:], ALU.add)
            nc.vector.tensor_scalar(cin_bk[:], small["cin_b"][:], float(K), None, ALU.mult).then_inc(zw_ready, 1)
            dve.wait_ge(table_loaded, 16 * (1 + len(picked)))
            for n, (_, _, table, parts, _, _) in enumerate(picked):
                for k in range(3):
                    last = nc.vector.tensor_copy(parts[:, :, k, :], table[:])
                    if k < 2:
                        last.then_inc(table_step, 1)
                        dve.wait_ge(table_step, 4 * n + 2 * k + 1)
                        nc.vector.tensor_tensor(table[:], table[:], parts[:, :, k, :], ALU.subtract
                                                ).then_inc(table_step, 1)
                        dve.wait_ge(table_step, 4 * n + 2 * k + 2)

            def make_hot(n):
                for _, vp, _, _, ids, hot in picked:
                    shape = [vp, SLICES, P]
                    last = nc.vector.tensor_tensor(
                        hot[:], ids[:, bass.ds(n * P, P)].unsqueeze(1).to_broadcast(shape),
                        numbers[0:vp, :].unsqueeze(2).to_broadcast(shape), ALU.is_equal)
                last.then_inc(hot_ready, 1)

            def add_parts(n, par):
                dve.wait_ge(hot_full, n + 1)
                for (f, *_), bank in zip(picked, mps):
                    last = nc.vector.tensor_reduce(
                        rows[par][:, f * K:(f + 1) * K], bank[:, HOT0:HOT0 + 3 * K].rearrange("b (s k) -> b k s", k=K),
                        mybir.AxisListType.X, ALU.add)
                last.then_inc(hot_rows, 1)

            dve.wait_ge(ids_loaded[0], 16 * len(picked))
            make_hot(0)
            dve.wait_ge(dense_loaded, 32)
            for n, (x, hi, lo) in enumerate(zip(dense, high, part)):
                minus = small["minus"][:, 2 * n:2 * n + 2]
                for k in range(2):
                    nc.vector.tensor_copy(hi[:], x[:]).then_inc(split_step, 1)
                    dve.wait_ge(split_step, 3 * n + 2 * k + 1)
                    last = nc.vector.scalar_tensor_tensor(lo[:] if k else x[:], hi[:], minus[:, k:k + 1], x[:],
                                                          ALU.mult, ALU.add)
                    if k == 0:
                        last.then_inc(split_step, 1)
                        dve.wait_ge(split_step, 3 * n + 2)
            last.then_inc(dense_ready, 1)

            def turn(it, par, g):
                f0, f1 = GROUPS[g]
                dve.wait_ge(gathered[par][g], (it + 1) * (16 * len(GATHERED[g])))
                if any(f0 <= f < f1 for f in PICKED):
                    dve.wait_ge(hot_rows, 2 * it + (par + 1))
                done = emb_ready[par] if f1 == F else turned[par][g]
                nc.vector.transpose(emb[par][:, :, f0:f1].rearrange("p u f -> p f u"),
                                    rows[par][:, f0 * K:f1 * K].rearrange("p (f k) -> p f k", k=K)).then_inc(done, 1)

            def products(it, par, g, h):
                if g == 0:
                    dve.wait_ge(half_used[h], 2 * it + (par + 1))
                if g < len(GROUPS) - 1:
                    dve.wait_ge(turned[par][g], it + 1)
                else:
                    dve.wait_ge(emb_ready[par], it + 2)
                e = emb[par][:, h * U_HALF:(h + 1) * U_HALF, :]
                q = prod[h]

                def rectangle(row, width, p0, np_, q0, nq, b0=0):
                    shape = [P, U_HALF, np_, nq]
                    return nc.vector.tensor_tensor(
                        q[:, :, row:row + np_ * width].rearrange("p u (a b) -> p u a b", b=width)[:, :, :, b0:b0 + nq],
                        e[:, :, p0:p0 + np_].unsqueeze(3).to_broadcast(shape),
                        e[:, :, q0:q0 + nq].unsqueeze(2).to_broadcast(shape), ALU.mult)

                def triangle(row, p0, np_):
                    for p in range(np_ - 1):
                        w = np_ - 1 - p
                        nc.vector.tensor_tensor(
                            q[:, :, row:row + w], e[:, :, p0 + p:p0 + p + 1].to_broadcast([P, U_HALF, w]),
                            e[:, :, p0 + p + 1:p0 + np_], ALU.mult)
                        row += w

                f0, f1 = GROUPS[g]
                squares, s_pairs, b_pairs = len(PART_A), len(PART_A) + F, ONE_ROW + 1
                nc.vector.tensor_tensor(q[:, :, squares + f0:squares + f1], e[:, :, f0:f1], e[:, :, f0:f1], ALU.mult)
                if g == 0:
                    nc.vector.tensor_copy(q[:, :, 0:HALF], e[:, :, 0:HALF])
                    rectangle(HALF, 8, 0, 5, 5, 8)
                    rectangle(HALF + 40, 3, 5, 5, 10, 3)
                    triangle(HALF + 55, 10, 3)
                    triangle(s_pairs, 0, 5)
                    triangle(s_pairs + 10, 5, 5)
                elif g == 1:
                    triangle(b_pairs + 42, 13, 6)
                elif g == 2:
                    triangle(s_pairs + 20, 19, 4)
                    rectangle(b_pairs, 7, 13, 6, 19, 4)
                else:
                    triangle(s_pairs + 26, 23, 3)
                    rectangle(b_pairs, 7, 13, 6, 23, 3, b0=4)
                    rectangle(b_pairs + 57, 3, 19, 4, 23, 3).then_inc(prod_ready[h], 1)

            def tile(it, par):
                add_parts(2 * it + par, par)
                for g in range(len(GROUPS)):
                    turn(it, par, g)
                    for h in range(2):
                        products(it, par, g, h)

            def tile_by_halves(par):
                add_parts(par, par)
                for g in range(len(GROUPS)):
                    turn(0, par, g)
                    products(0, par, g, 0)
                for g in range(len(GROUPS)):
                    products(0, par, g, 1)

            tile_by_halves(0)
            make_hot(1)
            dve.wait_ge(pre_free, PRE)
            step = 0
            for c in range(2):
                n = RN[c]
                v = V[0:n, V0[c] * H:(V0[c] + JN[c]) * H]
                m = small["mult"][0:n, V0[c]:V0[c] + JN[c]].unsqueeze(2).to_broadcast([n, JN[c], H])
                v3 = v.rearrange("r (j h) -> r j h", h=H)
                for t in range(2):
                    dve.wait_ge(v_gathered[c][t], 16)
                    nc.vector.tensor_tensor(v, v, other[c][t][0:n, :], ALU.add).then_inc(v_step, 1)
                    dve.wait_ge(v_step, step + t + 1)
                last = nc.vector.tensor_tensor(v3, v3, m, ALU.mult)
                if c == 0:
                    last.then_inc(v_ready, 1)
                    step += 2
                    continue
                last.then_inc(v_step, 1)
                dve.wait_ge(v_step, step + 3)
                lower, upper = (v3[:, f:f + 2 * len(PAIRED) - 1:2, :] for f in PAIRED[0])
                nc.vector.tensor_copy(upper[0:n - LOW], lower[LOW:n]).then_inc(v_ready, 1)
            tile_by_halves(1)
            dve.wait_ge(ids_loaded[1], 16 * len(picked))
            with dve.Fori(1, TILES // 2) as it:
                for par in range(2):
                    make_hot(2 * it + par)
                    tile(it, par)

        @block.scalar
        def _(act):
            def fill_mov(it, par, h, first):
                if first:
                    act.wait_ge(turned[par][0], it + 1)
                    act.wait_ge(half_used[h], 2 * it + (par + 1))
                else:
                    act.wait_ge(emb_ready[par], it + 2)
                f0, f1 = (0, HALF) if first else (HALF, F)
                for g in range(FOUR):
                    last = nc.scalar.copy(mov[h][g * K:(g + 1) * K, :, g, 1 + f0:1 + f1],
                                          emb[par][g * K:(g + 1) * K, h * U_HALF:(h + 1) * U_HALF, f0:f1])
                if not first:
                    last.then_inc(mov_ready[h], 1)

            def take_t(n, par, before=None):
                for k in range(16):
                    c, u0, bk = k % 2, k // 2 * EVAC, k % 4
                    if k % 8 == 7:
                        act.wait_ge(half_used[k // 8], n + 2)
                    elif bk == 3:
                        act.wait_ge(tps_full[bk], 2 * n + (k // 8 + 1))
                    else:
                        act.wait_ge(tps_full[bk], 4 * n + (k // 4 + 1))
                    src = tps[bk][0:RN[c], 0:EVAC * FOUR * MCOLS].rearrange("r (u g c) -> r c g u", g=FOUR, c=MCOLS)
                    src = src[:, C0[c]:C0[c] + CN[c], :, :]
                    dst = T[par][0:RN[c], T0[c]:T0[c] + CN[c], :].rearrange("r c (g u) -> r c g u", g=FOUR)
                    last = nc.scalar.copy(dst[:, :, :, u0:u0 + EVAC], src)
                    if c == 1:
                        for to, f in zip((0, LOW), PAIRED[0]):
                            src = tps[bk][LOW:RN[1], 0:EVAC * FOUR * MCOLS].rearrange(
                                "r (u g c) -> r c g u", g=FOUR, c=MCOLS)[:, 1 + f:2 * len(PAIRED) + f:2, :, :]
                            dst = T[par][to:to + RN[1] - LOW, TPAIR:, :].rearrange("r c (g u) -> r c g u", g=FOUR)
                            last = nc.scalar.copy(dst[:, :, :, u0:u0 + EVAC], src)
                    last.then_inc(tps_free[bk], 1)
                    if before is not None and k == TOP3_AT:
                        take_y(before)

            def take_z(n):
                for s in range(2):
                    act.wait_ge(z_full, 2 * n + (s + 1))
                    nc.scalar.activation(z[:, s, :], zps[s][:, 0:P], ACT.Identity,
                                         bias=cin_bk[:, s:s + 1]).then_inc(z_ready, 1)

            def take_h1(n):
                for s in range(4):
                    act.wait_ge(h_full, 7 * n + (s + 1))
                    nc.scalar.activation(h1[:, s, :], tps[s][:, 0:P], ACT.Relu,
                                         bias=small["b_top1"][:, s:s + 1]).then_inc(h_ready, 1)

            def take_h2(n):
                for s in range(2):
                    act.wait_ge(h_full, 7 * n + (s + 5))
                    nc.scalar.activation(h2[:, s, :], mps[s][:, 0:P], ACT.Relu,
                                         bias=small["b_top2"][:, s:s + 1]).then_inc(h_ready, 1)

            def take_y(n):
                act.wait_ge(h_full, 7 * n + 7)
                nc.scalar.copy(y[:, bass.ds(n * P, P)], zps[0][0:1, 0:P]).then_inc(h_ready, 1)

            def rest(n, following):
                for h in range(2):
                    fill_mov(*following, h, True)
                take_z(n)
                take_h1(n)
                fill_mov(*following, 0, False)
                take_h2(n)
                fill_mov(*following, 1, False)

            n = 0
            for s, (g, r0, r1) in enumerate(USTAGES):
                if s >= 4:
                    act.wait_ge(u_written[s % 4], 16 * len(UPARTS[s - 4]))
                for q, nq in UQ:
                    act.wait_ge(pre_full, n + 1)
                    nc.scalar.copy(stage[s % 4][0:r1 - r0, q * H:(q + nq) * H],
                                   tps[n % 4][0:r1 - r0, 0:nq * H]).then_inc(pre_free, 1)
                    n += 1
            act.wait_ge(preset, 1)
            for h in range(2):
                fill_mov(0, 0, h, True)
            for v, (c, j, nj) in enumerate(VSTEPS):
                if v == len(VSTEPS) - 2:
                    fill_mov(0, 0, 0, False)
                act.wait_ge(pre_full, n + 1)
                nc.scalar.copy(V[0:RN[c], (V0[c] + j) * H:(V0[c] + j + nj) * H],
                               tps[n % 4][0:RN[c], 0:nj * H]).then_inc(pre_free, 1)
                n += 1
            for bk in range(4):
                act.sem_inc(tps_free[bk], 1)
            act.wait_ge(zw_ready, 3)
            fill_mov(0, 0, 1, False)
            take_t(0, 0)
            act.wait_ge(top_loaded, 16 * len(TOP))
            rest(0, (0, 1))
            with act.Fori(0, TILES // 2 - 1) as it:
                for par in range(2):
                    take_t(2 * it + (par + 1), 1 - par, 2 * it + par)
                    rest(2 * it + (par + 1), (it + 1, par))
            take_t(TILES - 1, 1, TILES - 2)
            take_z(TILES - 1)
            take_h1(TILES - 1)
            take_h2(TILES - 1)
            take_y(TILES - 1)
            act.wait_ge(h_ready, 7 * TILES)
            act.dma_start(out.rearrange("b o -> o b"), y[:]).then_inc(y_stored, 16)
            act.wait_ge(y_stored, 16)

        @block.tensor
        def _(pe):
            for h in range(2):
                pe.sem_inc(half_used[h], 1)
            pe.wait_ge(w1f_ready, 1)

            def pick(n):
                pe.wait_ge(hot_ready, n + 1)
                for (_, _, _, parts, _, hot), bank in zip(picked, mps):
                    for s in range(SLICES):
                        last = nc.tensor.matmul(bank[:, HOT0:HOT0 + 3 * K], hot[:, s, :], parts[:, s, :, :],
                                                start=(s == 0), stop=(s == SLICES - 1))
                last.then_inc(hot_full, 1)

            n = 0
            for g, r0, r1 in USTAGES:
                if r0 == 0:
                    pe.wait_ge(w2_loaded[g], 16)
                if (g, r0) == HOT_AT:
                    pick(0)
                for q, nq in UQ:
                    if n >= 4:
                        pe.wait_ge(pre_free, n - 3)
                    first = (g * HALF + q) * H
                    nc.tensor.matmul(tps[n % 4][0:r1 - r0, 0:nq * H], w1f[:, g * HALF * F + r0:g * HALF * F + r1],
                                     w2[:, first:first + nq * H], start=True, stop=True).then_inc(pre_full, 1)
                    n += 1
            pe.wait_ge(w1r_ready, 1)
            for c, j, nj in VSTEPS:
                pe.wait_ge(pre_free, n - 3)
                nc.tensor.matmul(tps[n % 4][0:RN[c], 0:nj * H], small["w1a"][:, c * P:c * P + RN[c]],
                                 w2[:, (J0[c] + j) * H:(J0[c] + j + nj) * H], start=True, stop=True
                                 ).then_inc(pre_full, 1)
                n += 1
            pe.wait_ge(pre_free, PRE)
            pe.wait_ge(zw_ready, 3)

            def make_t(n, before=None, following=True):
                for h in range(2):
                    pe.wait_ge(mov_ready[h], n + 1)
                    pe.wait_ge(prod_ready[h], n + 1)
                    for k in range(8 * h, 8 * h + 8):
                        c, bk = k % 2, k % 4
                        pe.wait_ge(tps_free[bk], 4 * n + (k // 4 + 1))
                        w = FOUR * MCOLS
                        for v in range(EVAC):
                            u = k // 2 * EVAC + v - h * U_HALF
                            last = nc.tensor.matmul(
                                tps[bk][0:RN[c], v * w:(v + 1) * w], prod[h][:, u, R0[c]:R0[c] + RN[c]],
                                mov[h][:, u, :, :], start=True, stop=True)
                        last.then_inc(half_used[h] if k % 8 == 7 else tps_full[bk], 1)
                        if before is not None and k == TOP3_AT:
                            top3(before)
                        if following and k == PICK_AT:
                            pick(n + 1)

            def make_z(n, par):
                for c in range(2):
                    for bk in (c, c + 2):
                        pe.wait_ge(tps_free[bk], 4 * n + 5)
                    pe.wait_ge(v_ready, c + 1)
                    for n2, (j, col) in enumerate(Z2[c]):
                        if c == 1 and n2 == Z1_AT:
                            make_z1(n, par)
                        v = (V0[c] + j) * H
                        last = nc.tensor.matmul(zps[1][:, 0:P], V[0:RN[c], v:v + H], T[par][0:RN[c], col, :],
                                                start=(c == 0 and n2 == 0), stop=(c == 1 and n2 == len(Z2[1]) - 1))
                last.then_inc(z_full, 1)

            def make_z1(n, par):
                nc.tensor.matmul(zps[0][:, 0:P], small["z1a"][0:RN[0], 0:H], T[par][0:RN[0], TONE[0], :],
                                 start=True, stop=False)
                pe.wait_ge(across_ready, n * (16 * len(XQ)) + 16 * len(XQ))
                m = XQ[0][1] * HALF
                nc.tensor.matmul(zps[0][:, 0:P], small["xa"][0:m, 0:H], across[0:m, :], start=False, stop=False)
                nc.tensor.matmul(zps[0][:, 0:P], small["z1a"][0:RN[1], H:], T[par][0:RN[1], TONE[1], :],
                                 start=False, stop=True).then_inc(z_full, 1)

            def mlp(n):
                for s in range(4):
                    nc.tensor.matmul(tps[s][:, 0:P], part[1][:, s * P:(s + 1) * P], part[0][:, bass.ds(n * P, P)],
                                     start=True, stop=False)
                for k in range(2):
                    pe.wait_ge(z_ready, 2 * n + 1 + k)
                    for s in range(4):
                        last = nc.tensor.matmul(tps[s][:, 0:P], small["top1"][:, k * N1 + s * P:k * N1 + (s + 1) * P],
                                                z[:, k, :], start=False, stop=(k == 1))
                        if k == 1:
                            last.then_inc(h_full, 1)
                for k in range(4):
                    pe.wait_ge(h_ready, 7 * n + k + 1)
                    for m in range(2):
                        w = k * N2 + m * P
                        last = nc.tensor.matmul(mps[m][:, 0:P], small["top2"][:, w:w + P], h1[:, k, :],
                                                start=(k == 0), stop=(k == 3))
                        if k == 3:
                            last.then_inc(h_full, 1)

            def top3(n):
                for k in range(2):
                    pe.wait_ge(h_ready, 7 * n + k + 5)
                    last = nc.tensor.matmul(zps[0][0:1, 0:P], small["top3"][:, k:k + 1], h2[:, k, :],
                                            start=(k == 0), stop=(k == 1))
                last.then_inc(h_full, 1)

            make_t(0)
            make_z(0, 0)
            pe.wait_ge(dense_ready, 1)
            pe.wait_ge(top_loaded, 16 * len(TOP))
            mlp(0)
            with pe.Fori(0, TILES // 2 - 1) as it:
                for par in range(2):
                    n = 2 * it + (par + 1)
                    make_t(n, 2 * it + par)
                    make_z(n, 1 - par)
                    mlp(n)
            make_t(TILES - 1, TILES - 2, following=False)
            make_z(TILES - 1, 1)
            mlp(TILES - 1)
            top3(TILES - 1)


def by_rows(first, second):
    idx = np.zeros((2, 2, P), np.int64)
    is_pair = np.zeros((2, P), bool)
    for c in range(2):
        for r, row in enumerate(ROWS[R0[c]:R0[c] + RN[c]]):
            if row != "one" and row[0] != "single":
                idx[0, c, r], idx[1, c, r] = row
                is_pair[c, r] = True
    return idx[first], idx[second], is_pair


def kernel(**inputs):
    import concourse.bacc as bacc
    from concourse.bass_utils import run_bass_kernel_spmd

    a = {k: np.asarray(v) for k, v in inputs.items()}
    W1, W2 = a["L0_rec_W1"], a["L0_rec_W2"]
    mult, zmult, index = plan()
    one = np.array([[r < RN[c] and ROWS[R0[c] + r] == "one" for r in range(P)] for c in range(2)])
    arrays = {"ids": a["ids"], "w1": W1.reshape(H, F * F), "w2": W2.transpose(1, 2, 0).reshape(H, F * H),
              "mult": mult, "zmult": zmult, "vidx": index}
    for name, order in (("a", (0, 1)), ("b", (1, 0))):
        p, q, is_pair = by_rows(*order)
        rows = np.where(is_pair[None], W1[:, p, q], np.float32(0))
        arrays["z1" + name] = rows.transpose(2, 1, 0).reshape(P, 2 * H)
        if name == "a":
            rows = np.where(one[None], a["L0_rec_b1"][:, None, None], rows)
        arrays["w1" + name] = rows.reshape(H, 2 * P)
    for name, rows in (("xa", W1[:, :HALF, HALF:].transpose(2, 1, 0)), ("xb", W1[:, HALF:, :HALF].transpose(1, 2, 0))):
        x = np.zeros((P, 2, H), W1.dtype)
        for part, (q0, q1) in enumerate(XQ):
            x[:(q1 - q0) * HALF, part] = rows[q0:q1].reshape(-1, H)
        arrays[name] = x.reshape(P, 2 * H)
    arrays["cin_b"] = np.stack([a["L0_rec_b1"], a["L0_rec_b2"]], axis=1)
    arrays["b_top1"] = a["b_top1"].reshape(N1 // P, P).T
    arrays["b_top2"] = a["b_top2"].reshape(N2 // P, P).T
    arrays["top1"] = a["W_top1"][:2 * H].reshape(2, P, N1).transpose(1, 0, 2).reshape(P, 2 * N1)
    arrays["top1d"] = np.tile(a["W_top1"][2 * H:], (len(PARTS), 1))
    arrays["top2"] = a["W_top2"].reshape(N1 // P, P, N2).transpose(1, 0, 2).reshape(P, -1)
    arrays["top3"] = a["W_top3"].reshape(N2 // P, P).T
    arrays["dense"] = np.tile(a["dense_ctx"].T, (len(PARTS), 1))
    minus = np.array([[-float(pair[n] in want) for n in range(2) for want in ("ml", "l")] for pair in PARTS],
                     np.float32)
    arrays["minus"] = minus.repeat(D, axis=0)
    arrays["numbers"] = np.arange(P * SLICES, dtype=np.int32).reshape(P, SLICES)
    for f in PICKED:
        arrays[f"ids{f}"] = a["ids"][:, f].reshape(1, B)
    for f in range(F):
        arrays[f"tbl_{f}"] = a[f"tbl_{f}"]

    nc = bacc.Bacc("TRN2", target_bir_lowering=False, num_devices=1)
    maps, aps = {}, {}
    for name, x in arrays.items():
        x = np.ascontiguousarray(x)
        maps["in_" + name] = x
        aps[name] = nc.dram_tensor("in_" + name, x.shape, mybir.dt.from_np(x.dtype), kind="ExternalInput").ap()
    out = nc.dram_tensor("out", (B, 1), F32, kind="ExternalOutput").ap()
    build(nc, aps, [aps[f"tbl_{f}"] for f in range(F)], out)
    r = run_bass_kernel_spmd(nc, [maps], core_ids=[0])
    return r.results[0]["out"]
```
